# Optimizing a Trainium2 kernel written in Bass

```python
import numpy as np
import jax
import jax.numpy as jnp

def _softmax(x, axis=-1):
    return jax.nn.softmax(x, axis=axis)

def _gelu(x):
    return jax.nn.gelu(x, approximate=True)

def _silu(x):
    return jax.nn.silu(x)

def _sigmoid(x):
    return jax.nn.sigmoid(x)

def _layernorm(x, axis=-1, eps=1e-05):
    m = jnp.mean(x, axis=axis, keepdims=True)
    v = jnp.var(x, axis=axis, keepdims=True)
    return (x - m) / jnp.sqrt(v + eps)

def _scatter_add(tgt, idx, src, axis=0):
    return tgt.at[idx].add(src)

def _segment_sum(src, seg, n):
    return jax.ops.segment_sum(src, seg, n)
kernel_name = 'mk_seq_preln_d2_jaxref_r8_cfbb66'

def setup_inputs(seed: int=0):
    np.random.seed(seed)
    _w = jnp.asarray

    def _L0_attn_setup():
        import jax, jax.numpy as jnp
        import numpy as np
        N_HEADS = 16

        def _rotate_half(t):
            shp = t.shape
            t2 = t.reshape(*shp[:-1], shp[-1] // 2, 2)
            return jnp.stack((-t2[..., 1], t2[..., 0]), axis=-1).reshape(shp)
        key = jax.random.key(seed)
        k1, k2, k3 = jax.random.split(key, 3)
        B, N, D = (2, 256, 128)
        x = jax.random.normal(k1, (B, N, D), dtype=jnp.float32)
        w_qkv = jax.random.normal(k2, (D, 3 * D), dtype=jnp.float32) * D ** (-0.5)
        w_proj = jax.random.normal(k3, (D, D), dtype=jnp.float32) * D ** (-0.5)
        return {'x': x, 'w_qkv': w_qkv, 'w_proj': w_proj}
    _L0_attn_in = _L0_attn_setup()

    def _L0_ffn_setup():
        import jax, jax.numpy as jnp
        import numpy as np
        BLOCK = 16
        _GRID = jnp.array([0.0, 0.5, 1.0, 1.5, 2.0, 3.0, 4.0, 6.0], dtype=jnp.float32)
        _MID = jnp.array([0.25, 0.75, 1.25, 1.75, 2.5, 3.5, 5.0], dtype=jnp.float32)

        def fp4_quant_dequant(x):
            shape = x.shape
            xb = x.reshape(shape[:-1] + (shape[-1] // BLOCK, BLOCK))
            scale = jnp.max(jnp.abs(xb), axis=-1, keepdims=True) / 6.0
            scale = jnp.maximum(scale, jnp.float32(1e-12))
            xn = xb / scale
            idx = jnp.searchsorted(_MID, jnp.abs(xn))
            q = _GRID[idx] * jnp.sign(xn) * scale
            return q.reshape(shape)

        def fp4_linear(x, w):
            xq = fp4_quant_dequant(x)
            wq = fp4_quant_dequant(w)
            return jnp.einsum('bsk,nk->bsn', xq, wq)
        key = jax.random.key(seed)
        k1, k2, k3, k4 = jax.random.split(key, 4)
        H, I = (128, 352)
        x = jax.random.normal(k1, (4, 512, H), dtype=jnp.float32)
        w_gate = jax.random.normal(k2, (I, H), dtype=jnp.float32) * 0.02
        w_up = jax.random.normal(k3, (I, H), dtype=jnp.float32) * 0.02
        w_down = jax.random.normal(k4, (H, I), dtype=jnp.float32) * 0.02
        return {'x': x, 'w_gate': w_gate, 'w_up': w_up, 'w_down': w_down}
    _L0_ffn_in = _L0_ffn_setup()

    def _L1_attn_setup():
        import jax, jax.numpy as jnp
        import numpy as np
        D_MODEL = 128
        N_HEADS = 16
        D_K = D_MODEL // N_HEADS
        THETA = 10000.0
        BATCH = 1
        SEQ = 512

        def _rope(x, pos, inv_freq):
            angles = pos[:, None].astype(jnp.float32) * inv_freq
            cos = jnp.repeat(jnp.cos(angles), 2, axis=-1)
            sin = jnp.repeat(jnp.sin(angles), 2, axis=-1)
            x_rot = jnp.stack([-x[..., 1::2], x[..., 0::2]], axis=-1).reshape(x.shape)
            return x * cos + x_rot * sin
        key = jax.random.key(seed)
        ks = jax.random.split(key, 5)
        std = (2.0 / (D_MODEL + D_MODEL)) ** 0.5
        mk = lambda k: jax.random.truncated_normal(k, -3.0, 3.0, (D_MODEL, D_MODEL), jnp.float32) * std
        return {'x': jax.random.normal(ks[0], (BATCH, SEQ, D_MODEL), jnp.float32), 'Wq': mk(ks[1]), 'Wk': mk(ks[2]), 'Wv': mk(ks[3]), 'Wo': mk(ks[4])}
    _L1_attn_in = _L1_attn_setup()

    def _L1_ffn_setup():
        import jax, jax.numpy as jnp
        import numpy as np
        DIM = 128
        DEPTH = 6
        HEADS = 16
        DIM_HEAD = 64
        WINDOW = 32
        INNER = HEADS * DIM_HEAD
        DIM_INNER = int(DIM * 4 * 2 / 3)
        QK_SCALE = 8.0

        def shift_tokens(t):
            a, s = jnp.split(t, 2, -1)
            s = jnp.pad(s, ((0, 0), (1, 0), (0, 0)))[:, :-1]
            return jnp.concatenate([a, s], -1)

        def l2norm(t):
            return t / jnp.maximum(jnp.linalg.norm(t, axis=-1, keepdims=True), 1e-12)

        def rotate_half(x):
            x1, x2 = jnp.split(x, 2, -1)
            return jnp.concatenate([-x2, x1], -1)

        def rotary_tables(n):
            half = jnp.arange(0, DIM_HEAD, 2, dtype=jnp.float32)
            inv_freq = 1.0 / 10000.0 ** (half / DIM_HEAD)
            t = jnp.arange(n, dtype=jnp.float32)
            freqs = t[:, None] * inv_freq[None, :]
            freqs = jnp.concatenate([freqs, freqs], -1)
            base_scale = (half + 0.4 * DIM_HEAD) / (1.4 * DIM_HEAD)
            power = (t - n // 2) / (WINDOW // 2)
            scale = base_scale[None, :] ** power[:, None]
            scale = jnp.concatenate([scale, scale], -1)
            return (freqs, scale)

        def local_attention(q, k, v):
            b, h, n, d = q.shape
            w = WINDOW
            nw = n // w
            bq = q.reshape(b, h, nw, w, d)
            bk = k.reshape(b, h, nw, w, d)
            bv = v.reshape(b, h, nw, w, d)

            def look(t):
                p = jnp.pad(t, ((0, 0), (0, 0), (1, 0), (0, 0), (0, 0)))
                return jnp.concatenate([p[:, :, :nw], p[:, :, 1:]], axis=3)
            bk2, bv2 = (look(bk), look(bv))
            seq = jnp.arange(n).reshape(nw, w)
            seq_p = jnp.pad(seq, ((1, 0), (0, 0)), constant_values=-1)
            jt = jnp.concatenate([seq_p[:nw], seq_p[1:]], axis=1)
            it = seq[:, :, None]
            jb = jt[:, None, :]
            mask = (it < jb) | (it > jb + w) | (jb == -1)
            sim = jnp.einsum('bhwie,bhwje->bhwij', bq, bk2) * QK_SCALE
            sim = jnp.where(mask, -jnp.finfo(sim.dtype).max, sim)
            attn = jax.nn.softmax(sim, -1)
            out = jnp.einsum('bhwij,bhwje->bhwie', attn, bv2)
            return out.reshape(b, h, n, d)

        def attn_layer(x, Wqkv, qs, ksc, Wo):
            b, n, _ = x.shape
            qkv = x @ Wqkv
            q, k, v = jnp.split(qkv, 3, -1)
            sh = lambda t: t.reshape(b, n, HEADS, DIM_HEAD).transpose(0, 2, 1, 3)
            q, k, v = (sh(q), sh(k), sh(v))
            q = l2norm(q) * qs
            k = l2norm(k) * ksc
            freqs, scale = rotary_tables(n)
            cos, sin = (jnp.cos(freqs), jnp.sin(freqs))
            q = q * cos * scale + rotate_half(q) * sin * scale
            inv = 1.0 / scale
            k = k * cos * inv + rotate_half(k) * sin * inv
            out = local_attention(q, k, v)
            out = out.transpose(0, 2, 1, 3).reshape(b, n, INNER)
            return out @ Wo

        def ffn_layer(x, g, bln, W1, b1, W2, b2):
            mu = x.mean(-1, keepdims=True)
            var = ((x - mu) ** 2).mean(-1, keepdims=True)
            xn = (x - mu) / jnp.sqrt(var + 1e-05) * g + bln
            hg = xn @ W1 + b1
            a, gate = jnp.split(hg, 2, -1)
            return a * jax.nn.gelu(gate, approximate=False) @ W2 + b2
        key = jax.random.key(seed)
        ks = jax.random.split(key, 8)
        B, N = (2, 256)
        init = lambda k, shape: jax.random.normal(k, shape, jnp.float32) * 0.02
        return {'x': jax.random.normal(ks[0], (B, N, DIM), jnp.float32), 'Wqkv': init(ks[1], (DEPTH, DIM, 3 * INNER)), 'q_scale': jnp.ones((DEPTH, DIM_HEAD), jnp.float32), 'k_scale': jnp.ones((DEPTH, DIM_HEAD), jnp.float32), 'Wo': init(ks[2], (DEPTH, INNER, DIM)), 'ln_g': jnp.ones((DEPTH, DIM), jnp.float32), 'ln_b': jnp.zeros((DEPTH, DIM), jnp.float32), 'W1': init(ks[3], (DEPTH, DIM, 2 * DIM_INNER)), 'b1': jnp.zeros((DEPTH, 2 * DIM_INNER), jnp.float32), 'W2': init(ks[4], (DEPTH, DIM_INNER, DIM)), 'b2': jnp.zeros((DEPTH, DIM), jnp.float32)}
    _L1_ffn_in = _L1_ffn_setup()
    _d = {'L0_attn_x': _L0_attn_in['x'], 'L0_attn_w_qkv': _L0_attn_in['w_qkv'], 'L0_attn_w_proj': _L0_attn_in['w_proj'], 'L0_ffn_w_gate': _L0_ffn_in['w_gate'], 'L0_ffn_w_up': _L0_ffn_in['w_up'], 'L0_ffn_w_down': _L0_ffn_in['w_down'], 'L1_attn_Wq': _L1_attn_in['Wq'], 'L1_attn_Wk': _L1_attn_in['Wk'], 'L1_attn_Wv': _L1_attn_in['Wv'], 'L1_attn_Wo': _L1_attn_in['Wo'], 'L1_ffn_Wqkv': _L1_ffn_in['Wqkv'], 'L1_ffn_q_scale': _L1_ffn_in['q_scale'], 'L1_ffn_k_scale': _L1_ffn_in['k_scale'], 'L1_ffn_Wo': _L1_ffn_in['Wo'], 'L1_ffn_ln_g': _L1_ffn_in['ln_g'], 'L1_ffn_ln_b': _L1_ffn_in['ln_b'], 'L1_ffn_W1': _L1_ffn_in['W1'], 'L1_ffn_b1': _L1_ffn_in['b1'], 'L1_ffn_W2': _L1_ffn_in['W2'], 'L1_ffn_b2': _L1_ffn_in['b2']}
    _x0 = _d['L0_attn_x']
    _d['L0_attn_x'] = jax.random.normal(jax.random.fold_in(jax.random.key(seed), 1), (1, 2048, 128), dtype=_x0.dtype)
    del _x0
    return _d

def reference(L0_attn_x, L0_attn_w_qkv, L0_attn_w_proj, L0_ffn_w_gate, L0_ffn_w_up, L0_ffn_w_down, L1_attn_Wq, L1_attn_Wk, L1_attn_Wv, L1_attn_Wo, L1_ffn_Wqkv, L1_ffn_q_scale, L1_ffn_k_scale, L1_ffn_Wo, L1_ffn_ln_g, L1_ffn_ln_b, L1_ffn_W1, L1_ffn_b1, L1_ffn_W2, L1_ffn_b2):

    def _L0_attn_ref(x, w_qkv, w_proj):
        import jax, jax.numpy as jnp
        import numpy as np
        N_HEADS = 16

        def _rotate_half(t):
            shp = t.shape
            t2 = t.reshape(*shp[:-1], shp[-1] // 2, 2)
            return jnp.stack((-t2[..., 1], t2[..., 0]), axis=-1).reshape(shp)
        B, N, D = x.shape
        H = N_HEADS
        hd = D // H
        qkv = x @ w_qkv
        qkv = qkv.reshape(B, N, 3, H, hd).transpose(2, 0, 3, 1, 4)
        q, k, v = (qkv[0], qkv[1], qkv[2])
        inv_freq = 1.0 / 10000.0 ** (jnp.arange(0, hd, 2, dtype=jnp.float32) / hd)
        freqs = jnp.arange(N, dtype=jnp.float32)[:, None] * inv_freq[None, :]
        sin = jnp.repeat(jnp.sin(freqs), 2, axis=-1)[None, None]
        cos = jnp.repeat(jnp.cos(freqs), 2, axis=-1)[None, None]
        q = q * cos + _rotate_half(q) * sin
        k = k * cos + _rotate_half(k) * sin
        scale = hd ** (-0.5)
        attn = jax.nn.softmax(jnp.einsum('bhqd,bhkd->bhqk', q, k) * scale, axis=-1)
        out = jnp.einsum('bhqk,bhkd->bhqd', attn, v)
        out = out.transpose(0, 2, 1, 3).reshape(B, N, D)
        return out @ w_proj

    def _L0_ffn_ref(x, w_gate, w_up, w_down):
        import jax, jax.numpy as jnp
        import numpy as np
        BLOCK = 16
        _GRID = jnp.array([0.0, 0.5, 1.0, 1.5, 2.0, 3.0, 4.0, 6.0], dtype=jnp.float32)
        _MID = jnp.array([0.25, 0.75, 1.25, 1.75, 2.5, 3.5, 5.0], dtype=jnp.float32)

        def fp4_quant_dequant(x):
            shape = x.shape
            xb = x.reshape(shape[:-1] + (shape[-1] // BLOCK, BLOCK))
            scale = jnp.max(jnp.abs(xb), axis=-1, keepdims=True) / 6.0
            scale = jnp.maximum(scale, jnp.float32(1e-12))
            xn = xb / scale
            idx = jnp.searchsorted(_MID, jnp.abs(xn))
            q = _GRID[idx] * jnp.sign(xn) * scale
            return q.reshape(shape)

        def fp4_linear(x, w):
            xq = fp4_quant_dequant(x)
            wq = fp4_quant_dequant(w)
            return jnp.einsum('bsk,nk->bsn', xq, wq)
        gate = fp4_linear(x, w_gate)
        y = fp4_linear(x, w_up)
        h = jax.nn.silu(gate) * y
        return fp4_linear(h, w_down)

    def _L1_attn_ref(x, Wq, Wk, Wv, Wo):
        import jax, jax.numpy as jnp
        import numpy as np
        D_MODEL = 128
        N_HEADS = 16
        D_K = D_MODEL // N_HEADS
        THETA = 10000.0
        BATCH = 1
        SEQ = 512

        def _rope(x, pos, inv_freq):
            angles = pos[:, None].astype(jnp.float32) * inv_freq
            cos = jnp.repeat(jnp.cos(angles), 2, axis=-1)
            sin = jnp.repeat(jnp.sin(angles), 2, axis=-1)
            x_rot = jnp.stack([-x[..., 1::2], x[..., 0::2]], axis=-1).reshape(x.shape)
            return x * cos + x_rot * sin
        b, s, _ = x.shape
        h, dk = (N_HEADS, D_K)
        proj = lambda W: jnp.einsum('bsi,oi->bso', x, W).reshape(b, s, h, dk).transpose(0, 2, 1, 3)
        q = proj(Wq)
        k = proj(Wk)
        v = proj(Wv)
        pos = jnp.arange(s)
        inv_freq = 1.0 / THETA ** (jnp.arange(0, dk, 2, dtype=jnp.float32) / dk)
        q = _rope(q, pos, inv_freq)
        k = _rope(k, pos, inv_freq)
        scores = jnp.einsum('bhqd,bhkd->bhqk', q, k) / jnp.sqrt(jnp.asarray(dk, jnp.float32))
        causal_mask = jnp.arange(s)[None, :] > jnp.arange(s)[:, None]
        scores = jnp.where(causal_mask, -jnp.inf, scores)
        weights = jax.nn.softmax(scores, axis=-1)
        out = jnp.einsum('bhqk,bhkd->bhqd', weights, v)
        out = out.transpose(0, 2, 1, 3).reshape(b, s, h * dk)
        return jnp.einsum('bsi,oi->bso', out, Wo)

    def _L1_ffn_ref(x, Wqkv, q_scale, k_scale, Wo, ln_g, ln_b, W1, b1, W2, b2):
        import jax, jax.numpy as jnp
        import numpy as np
        DIM = 128
        DEPTH = 6
        HEADS = 16
        DIM_HEAD = 64
        WINDOW = 32
        INNER = HEADS * DIM_HEAD
        DIM_INNER = int(DIM * 4 * 2 / 3)
        QK_SCALE = 8.0

        def shift_tokens(t):
            a, s = jnp.split(t, 2, -1)
            s = jnp.pad(s, ((0, 0), (1, 0), (0, 0)))[:, :-1]
            return jnp.concatenate([a, s], -1)

        def l2norm(t):
            return t / jnp.maximum(jnp.linalg.norm(t, axis=-1, keepdims=True), 1e-12)

        def rotate_half(x):
            x1, x2 = jnp.split(x, 2, -1)
            return jnp.concatenate([-x2, x1], -1)

        def rotary_tables(n):
            half = jnp.arange(0, DIM_HEAD, 2, dtype=jnp.float32)
            inv_freq = 1.0 / 10000.0 ** (half / DIM_HEAD)
            t = jnp.arange(n, dtype=jnp.float32)
            freqs = t[:, None] * inv_freq[None, :]
            freqs = jnp.concatenate([freqs, freqs], -1)
            base_scale = (half + 0.4 * DIM_HEAD) / (1.4 * DIM_HEAD)
            power = (t - n // 2) / (WINDOW // 2)
            scale = base_scale[None, :] ** power[:, None]
            scale = jnp.concatenate([scale, scale], -1)
            return (freqs, scale)

        def local_attention(q, k, v):
            b, h, n, d = q.shape
            w = WINDOW
            nw = n // w
            bq = q.reshape(b, h, nw, w, d)
            bk = k.reshape(b, h, nw, w, d)
            bv = v.reshape(b, h, nw, w, d)

            def look(t):
                p = jnp.pad(t, ((0, 0), (0, 0), (1, 0), (0, 0), (0, 0)))
                return jnp.concatenate([p[:, :, :nw], p[:, :, 1:]], axis=3)
            bk2, bv2 = (look(bk), look(bv))
            seq = jnp.arange(n).reshape(nw, w)
            seq_p = jnp.pad(seq, ((1, 0), (0, 0)), constant_values=-1)
            jt = jnp.concatenate([seq_p[:nw], seq_p[1:]], axis=1)
            it = seq[:, :, None]
            jb = jt[:, None, :]
            mask = (it < jb) | (it > jb + w) | (jb == -1)
            sim = jnp.einsum('bhwie,bhwje->bhwij', bq, bk2) * QK_SCALE
            sim = jnp.where(mask, -jnp.finfo(sim.dtype).max, sim)
            attn = jax.nn.softmax(sim, -1)
            out = jnp.einsum('bhwij,bhwje->bhwie', attn, bv2)
            return out.reshape(b, h, n, d)

        def attn_layer(x, Wqkv, qs, ksc, Wo):
            b, n, _ = x.shape
            qkv = x @ Wqkv
            q, k, v = jnp.split(qkv, 3, -1)
            sh = lambda t: t.reshape(b, n, HEADS, DIM_HEAD).transpose(0, 2, 1, 3)
            q, k, v = (sh(q), sh(k), sh(v))
            q = l2norm(q) * qs
            k = l2norm(k) * ksc
            freqs, scale = rotary_tables(n)
            cos, sin = (jnp.cos(freqs), jnp.sin(freqs))
            q = q * cos * scale + rotate_half(q) * sin * scale
            inv = 1.0 / scale
            k = k * cos * inv + rotate_half(k) * sin * inv
            out = local_attention(q, k, v)
            out = out.transpose(0, 2, 1, 3).reshape(b, n, INNER)
            return out @ Wo

        def ffn_layer(x, g, bln, W1, b1, W2, b2):
            mu = x.mean(-1, keepdims=True)
            var = ((x - mu) ** 2).mean(-1, keepdims=True)
            xn = (x - mu) / jnp.sqrt(var + 1e-05) * g + bln
            hg = xn @ W1 + b1
            a, gate = jnp.split(hg, 2, -1)
            return a * jax.nn.gelu(gate, approximate=False) @ W2 + b2
        for i in range(DEPTH):
            x = attn_layer(shift_tokens(x), Wqkv[i], q_scale[i], k_scale[i], Wo[i]) + x
            x = ffn_layer(shift_tokens(x), ln_g[i], ln_b[i], W1[i], b1[i], W2[i], b2[i]) + x
        return x
    x = L0_attn_x
    x = x + _L0_attn_ref(_layernorm(x, axis=-1), L0_attn_w_qkv, L0_attn_w_proj)
    x = x + _L0_ffn_ref(_layernorm(x, axis=-1), L0_ffn_w_gate, L0_ffn_w_up, L0_ffn_w_down)
    x = x + _L1_attn_ref(_layernorm(x, axis=-1), L1_attn_Wq, L1_attn_Wk, L1_attn_Wv, L1_attn_Wo)
    x = x + _L1_ffn_ref(_layernorm(x, axis=-1), L1_ffn_Wqkv, L1_ffn_q_scale, L1_ffn_k_scale, L1_ffn_Wo, L1_ffn_ln_g, L1_ffn_ln_b, L1_ffn_W1, L1_ffn_b1, L1_ffn_W2, L1_ffn_b2)
    return x

_drawn_inputs = setup_inputs


def setup_inputs(seed=0):
    import zlib

    import numpy as np

    out = dict(_drawn_inputs(seed))
    spreads = {'L1_ffn_q_scale': (1.0, 0.6),
     'L1_ffn_k_scale': (1.0, 0.6),
     'L1_ffn_ln_g': (1.0, 0.6),
     'L1_ffn_ln_b': (0.0, 0.8),
     'L1_ffn_b1': (0.0, 0.8),
     'L1_ffn_b2': (0.0, 0.1)}
    factors = {'L0_ffn_w_gate': 5.432,
     'L0_ffn_w_up': 5.165,
     'L0_ffn_w_down': 5.173,
     'L1_ffn_W1': 3.656,
     'L1_ffn_W2': 3.586}
    for name, (base, spread) in spreads.items():
        noise = np.random.default_rng([zlib.crc32(name.encode()), seed]).standard_normal(out[name].shape)
        drawn = base * np.exp(spread * noise) if base else spread * noise
        out[name] = jnp.asarray(drawn.astype(out[name].dtype))
    for name, factor in factors.items():
        out[name] = (out[name] * factor).astype(out[name].dtype)
    return out
```

```python
from collections import namedtuple
from contextlib import ExitStack

import concourse.bass as bass
from concourse import mybir

F32 = mybir.dt.float32
BF16 = mybir.dt.bfloat16
ALU = mybir.AluOpType
ACT = mybir.ActivationFunctionType
AX = mybir.AxisListType

P = 128
N = 2048
NT = N // P
CH = 512
NC = N // CH
TC = CH // P
H = 16
EPS = 1e-5

HD = P // H
G = 4
NG = H // G
VW = HD + 1
TERMS = [(0, 0), (0, 1), (0, 2), (1, 0), (1, 1), (2, 0)]
MROW = HD * len(TERMS)
KB = 4
LEAD = 3
ONES = 1.0019378662109375


def layer_norm(nc, t, x, xn, sq, s, n):
    def vector(e):
        e.tensor_reduce(t.stat[:, 0:n], x, AX.X, ALU.add).then_inc(s.ln_v, 1)
        e.wait_ge(s.ln_v, 1)
        e.tensor_scalar(t.stat[:, 16:16 + n], t.stat[:, 0:n], -1.0 / P, None, ALU.mult).then_inc(s.ln_v, 1)
        e.wait_ge(s.ln_v, 2)
        e.tensor_tensor(xn, x, t.stat[:, 16:16 + n].unsqueeze(2).to_broadcast([P, n, P]), ALU.add).then_inc(s.ln_v, 1)
        e.wait_ge(s.ln_a, 1)
        e.tensor_reduce(t.stat[:, 0:n], sq, AX.X, ALU.add).then_inc(s.ln_v, 1)
        e.wait_ge(s.ln_v, 4)
        e.tensor_scalar(t.stat[:, 16:16 + n], t.stat[:, 0:n], 1.0 / P, EPS, ALU.mult, ALU.add).then_inc(s.ln_v, 1)
        e.wait_ge(s.ln_a, 2)
        e.reciprocal(t.stat[:, 0:n], t.stat[:, 32:32 + n]).then_inc(s.ln_v, 1)
        e.wait_ge(s.ln_v, 6)
        e.tensor_tensor(xn, xn, t.stat[:, 0:n].unsqueeze(2).to_broadcast([P, n, P]), ALU.mult).then_inc(s.ln_v, 1)

    def scalar(e):
        e.wait_ge(s.ln_v, 3)
        e.activation(sq, xn, ACT.Square).then_inc(s.ln_a, 1)
        e.wait_ge(s.ln_v, 5)
        e.activation(t.stat[:, 32:32 + n], t.stat[:, 16:16 + n], ACT.Sqrt).then_inc(s.ln_a, 1)

    return vector, scalar


class Names:
    pass


def semaphores(ctx, nc, prefix, names):
    return namedtuple("Semaphores", names)(*[ctx.enter_context(nc.semaphore(prefix + name)) for name in names.split()])


def attention_inputs(nc, t, prefix, d, wq_dram, wo_dram, out_by_in):
    with ExitStack() as ctx:
        s = semaphores(ctx, nc, prefix, "ln_v ln_a load xT xT_a xT_b wT wall wprep proj rot split v v_set store")
        xn = ctx.enter_context(nc.sbuf_tensor(prefix + "xn", [P, NT, P], F32))
        sq = ctx.enter_context(nc.sbuf_tensor(prefix + "sq", [P, NT, P], F32))
        xT = ctx.enter_context(nc.sbuf_tensor(prefix + "xT", [P, N], F32))
        cos = ctx.enter_context(nc.sbuf_tensor(prefix + "cos", [P, N], F32))
        sin = ctx.enter_context(nc.sbuf_tensor(prefix + "sin", [P, N], F32))
        rot = ctx.enter_context(nc.sbuf_tensor(prefix + "rot", [P, 2, N], F32))
        piece = ctx.enter_context(nc.sbuf_tensor(prefix + "piece", [P, 6, N], BF16))
        wraw = ctx.enter_context(nc.sbuf_tensor(prefix + "wraw", [P, 4, P], F32))
        wall = ctx.enter_context(nc.sbuf_tensor(prefix + "wall", [P, 3, P], F32))
        wrot = ctx.enter_context(nc.sbuf_tensor(prefix + "wrot", [P, 2, P], F32))
        ps = t.ps
        ln_vector, ln_scalar = layer_norm(nc, t, t.x[:, :, :], xn[:, :, :], sq[:, :, :], s, NT)

        with nc.Block() as block:
            @block.sync
            def _(e):
                for i, w in enumerate(wq_dram):
                    e.dma_start(wraw[:, i, :], w).then_inc(s.load, 16)
                e.dma_start(wraw[:, 3, :], wo_dram).then_inc(s.load, 16)
                e.dma_start(cos[:, :], d.rope_cos).then_inc(s.load, 16)
                e.dma_start(sin[:, :], d.rope_sin).then_inc(s.load, 16)
                for i in range(2):
                    for j in range(3):
                        e.wait_ge(s.split, 5 * i + (1, 3, 5)[j])
                        e.dma_start(d.pieces[i, j], piece[:, 3 * i + j, :]).then_inc(s.store, 16)
                e.wait_ge(s.store, 96)

            @block.tensor
            def _(e):
                if out_by_in:
                    e.wait_ge(s.load, 96)
                    for i in range(4):
                        e.transpose(ps[:, 4, i * P:(i + 1) * P], wraw[:, i, :], t.ident[:, :]).then_inc(s.wT, 1)
                e.wait_ge(s.ln_v, 7)
                for i in range(NT):
                    e.transpose(ps[:, i // TC, (i % TC) * P:(i % TC + 1) * P], xn[:, i, :], t.ident[:, :]).then_inc(s.xT, 1)
                e.wait_ge(s.xT_a, 1)
                e.wait_ge(s.xT_b, 1)
                e.wait_ge(s.wprep, 5)
                for i in range(2):
                    if i:
                        e.wait_ge(s.rot, 2)
                    for c in range(NC):
                        e.matmul(ps[:, c, :], wall[:, i, :], xT[:, c * CH:(c + 1) * CH], start=True, stop=True)\
                            .then_inc(s.proj, 1)
                    for c in range(NC):
                        e.matmul(ps[:, 4 + c, :], wrot[:, i, :], xT[:, c * CH:(c + 1) * CH], start=True, stop=True)\
                            .then_inc(s.proj, 1)
                e.wait_ge(s.rot, 4)
                for i in range(NT):
                    e.matmul(ps[:, i // TC, (i % TC) * P:(i % TC + 1) * P], xT[:, i * P:(i + 1) * P], wall[:, 2, :],
                             start=True, stop=True).then_inc(s.v, 1)

            @block.vector
            def _(e):
                ln_vector(e)
                if out_by_in:
                    e.wait_ge(s.wT, 4)
                    w = ps[:, 4, :].rearrange("p (i n) -> p i n", i=4)
                else:
                    e.wait_ge(s.load, 96)
                    w = wraw
                e.tensor_scalar(wall[:, 0, :], w[:, 0, :], HD ** -0.5, None, ALU.mult).then_inc(s.wprep, 1)
                e.tensor_copy(wall[:, 1:3, :], w[:, 1:3, :]).then_inc(s.wprep, 1)
                e.tensor_copy(t.wo[:, :], w[:, 3, :]).then_inc(s.wprep, 1)
                e.wait_ge(s.wprep, 3)
                pair = lambda a: a.rearrange("p i (n two) -> p i n two", two=2)
                e.tensor_scalar(pair(wrot[:, :, :])[:, :, :, 0], pair(wall[:, 0:2, :])[:, :, :, 1], -1.0, None,
                                ALU.mult).then_inc(s.wprep, 1)
                e.tensor_copy(pair(wrot[:, :, :])[:, :, :, 1], pair(wall[:, 0:2, :])[:, :, :, 0]).then_inc(s.wprep, 1)
                e.wait_ge(s.xT, 8)
                e.tensor_copy(xT[:, 0:N // 2], ps[:, 0:2, :].rearrange("p b n -> p (b n)")).then_inc(s.xT_a, 1)
                for i in range(2):
                    e.wait_ge(s.proj, 8 * i + 4)
                    if i:
                        e.wait_ge(s.split, 5)
                    e.tensor_tensor(rot[:, 0, :], ps[:, 0:4, :].rearrange("p b n -> p (b n)"), cos[:, :], ALU.mult)\
                        .then_inc(s.rot, 1)
                    e.wait_ge(s.proj, 8 * i + 8)
                    e.tensor_tensor(rot[:, 1, :], ps[:, 4:8, :].rearrange("p b n -> p (b n)"), sin[:, :], ALU.mult)\
                        .then_inc(s.rot, 1)
                    e.wait_ge(s.rot, 2 * i + 2)
                    e.tensor_tensor(rot[:, 0, :], rot[:, 0, :], rot[:, 1, :], ALU.add).then_inc(s.wall, 1)
                    e.wait_ge(s.wall, i + 1)
                    for j in range(3):
                        e.tensor_copy(piece[:, 3 * i + j, :], rot[:, 0, :]).then_inc(s.split, 1)
                        if j < 2:
                            e.wait_ge(s.split, 5 * i + 2 * j + 1)
                            e.tensor_tensor(rot[:, 0, :], rot[:, 0, :], piece[:, 3 * i + j, :], ALU.subtract)\
                                .then_inc(s.split, 1)
                            e.wait_ge(s.split, 5 * i + 2 * j + 2)

            @block.scalar
            def _(e):
                ln_scalar(e)
                e.wait_ge(s.xT, NT)
                e.copy(xT[:, N // 2:N], ps[:, 2:4, :].rearrange("p b n -> p (b n)")).then_inc(s.xT_b, 1)
                e.wait_ge(s.v, NT)
                e.wait_ge(s.v_set, 1)
                for b in range(NC):
                    e.copy(t.V[:, TC * b:TC * b + TC, 0:H * VW].rearrange("p t (h w) -> p t h w", w=VW)[:, :, :, 0:HD],
                           ps[:, b, :].rearrange("p (t h d) -> p t h d", t=TC, d=HD)).then_inc(s.xT_b, 1)

            @block.gpsimd
            def _(e):
                e.memset(t.V[:, :, :], 1.0).then_inc(s.v_set, 1)


def attention(nc, t, prefix, d, causal):
    units = [(c, g) for c in range(NC) for g in range(NG)]
    tiles_of = lambda c: TC * (c + 1) if causal else NT
    blocks_of = lambda c: c + 1 if causal else KB

    def max_blocks(u):
        c, g = units[u]
        out = []
        for qt in range(TC):
            for h in range(G):
                for b in range(blocks_of(c)):
                    last = causal and b == c
                    out.append((qt, h, b, P * (qt + 1) if last else CH, last))
        return out

    first_max = [0]
    first_step = [0]
    for u, (c, _) in enumerate(units):
        first_max.append(first_max[-1] + len(max_blocks(u)))
        first_step.append(first_step[-1] + tiles_of(c))

    plan = [[] for _ in range(first_step[-1])]
    start = []
    completes = {}
    for u in range(1, len(units)):
        blocks = list(enumerate(max_blocks(u)))
        at, until = first_step[u - 1] - LEAD, first_step[u] - LEAD
        for k, x in blocks:
            step = at + k * (until - at) // len(blocks)
            (plan[step] if step >= 0 else start).append((u, k, x))
        completes[until - 1] = u

    def quarter(step, i):
        blocks = plan[step]
        return blocks[len(blocks) * i // 4:len(blocks) * (i + 1) // 4]

    with ExitStack() as ctx:
        s = semaphores(ctx, nc, prefix, "fill stack_k0 stack_k1 stack_k2 stack_k3 stack_q0 stack_q1 stack_q2 stack_q3 scored reduced nmax split mrow_even mrow_odd st_ready exp_done pv_done os_done "
                       "misc_ready misc_used onorm rcp oT")
        stack_k = [s.stack_k0, s.stack_k1, s.stack_k2, s.stack_k3]
        stack_q = [s.stack_q0, s.stack_q1, s.stack_q2, s.stack_q3]
        mrow_stored = [s.mrow_even, s.mrow_odd]
        sb = lambda name, shape, dt=F32: ctx.enter_context(nc.sbuf_tensor(prefix + name, shape, dt))
        QS = sb("QS", [P, NC, H, CH], BF16)
        KS = sb("KS", [P, H, N], BF16)
        Pb = sb("Pb", [P, 2, G, CH])
        OS = sb("OS", [P, 2, CH])
        part = sb("part", [P, 2, G * TC, KB])
        nmax = sb("nmax", [P, 2, G * TC])
        mrow = sb("mrow", [G * TC, 2, 2, P], BF16)
        rcp = sb("rcp", [P, 2, TC * G])
        o_tok = sb("o_tok", [P, 2, TC, P])
        oT = sb("oT", [P, 2, CH])
        ps = t.ps
        O, MISC = ps[:, 6, :], ps[:, 7, :]

        with nc.Block() as block:
            @block.sync
            def _(e):
                def stack_keys(g):
                    heads = slice(G * g, G * (g + 1))
                    for j in range(len(TERMS)):
                        e.dma_start(KS[HD * j:HD * (j + 1), heads, :],
                                    d.pieces[1, TERMS[j][1]].rearrange("(h d) n -> d h n", d=HD)[:, heads, :])\
                            .then_inc(stack_k[g], 16)

                def stack_queries(c):
                    for j in range(len(TERMS)):
                        e.dma_start(QS[HD * j:HD * (j + 1), c, :, :],
                                    d.pieces[0, TERMS[j][0], :, c * CH:(c + 1) * CH].rearrange("(h d) n -> d h n", d=HD))\
                            .then_inc(stack_q[c], 16)

                e.wait_ge(s.fill, 2)
                stack_keys(0)
                stack_queries(0)
                for g in range(1, NG):
                    stack_keys(g)
                for c in range(1, NC):
                    stack_queries(c)
                for u, (c, g) in enumerate(units):
                    e.wait_ge(s.split, 2 * u + 2)
                    for j in range(2):
                        e.dma_start(QS[MROW + j:MROW + j + 1, c, G * g:G * g + G, :].rearrange("p h n -> p (h n)"),
                                    mrow[:, u % 2, j, :]).then_inc(mrow_stored[u % 2], 16)

            @block.gpsimd
            def _(e):
                e.memset(QS[:, :, :, :].rearrange("p c h n -> p (c h n)").bitcast(F32), 0.0).then_inc(s.fill, 1)

            @block.tensor
            def _(e):
                misc = 0

                def max_block(u, k, qt, h, b, width, masked):
                    c, g = units[u]
                    n = first_max[u] + k
                    if k == 0 and c == 0:
                        e.wait_ge(stack_k[g], 16 * len(TERMS))
                    if k == 0 and g == 0:
                        e.wait_ge(stack_q[c], 16 * len(TERMS))
                    if n >= 2:
                        e.wait_ge(s.reduced, n - 1)
                    bank = ps[:, 4 + n % 2, :]
                    head = G * g + h
                    if masked:
                        e.matmul(bank[:, width - P:width], t.identb[:, :], t.mask_qk[:, :], start=True, stop=False,
                                 skip_group_check=True)
                    mm = e.matmul(bank[:, 0:width], QS[:, c, head, qt * P:(qt + 1) * P],
                                  KS[:, head, b * CH:b * CH + width], start=not masked, stop=True,
                                  skip_group_check=masked)
                    mm.then_inc(s.scored, 1)

                def max_rows(u):
                    nonlocal misc
                    e.wait_ge(s.nmax, u + 1)
                    if misc:
                        e.wait_ge(s.misc_used, misc)
                    e.transpose(MISC[0:G * TC, 0:P], nmax[:, u % 2, :], t.ident[:, :]).then_inc(s.misc_ready, 1)
                    misc += 1

                def out_rows(u):
                    nonlocal misc
                    e.wait_ge(s.os_done, u + 1)
                    e.wait_ge(s.misc_used, misc)
                    for qt in range(TC):
                        tr = e.transpose(MISC[:, qt * P:(qt + 1) * P], OS[:, u % 2, qt * P:(qt + 1) * P], t.ident[:, :])
                    tr.then_inc(s.misc_ready, 1)
                    misc += 1

                def chunk_columns(c):
                    nonlocal misc
                    e.wait_ge(s.onorm, NG * (c + 1))
                    e.wait_ge(s.misc_used, misc)
                    for qt in range(TC):
                        tr = e.transpose(MISC[:, qt * P:(qt + 1) * P], o_tok[:, c % 2, qt, :], t.ident[:, :])
                    tr.then_inc(s.misc_ready, 1)
                    misc += 1

                def chunk_project(c):
                    nonlocal misc
                    e.wait_ge(s.misc_used, misc)
                    for qt in range(TC):
                        mm = e.matmul(MISC[:, qt * P:(qt + 1) * P], oT[:, c % 2, qt * P:(qt + 1) * P], t.wo[:, :],
                                      start=True, stop=True)
                    mm.then_inc(s.misc_ready, 1)
                    misc += 1

                def first_column(u, kt):
                    c = units[u][0]
                    return P * (kt - TC * c) if causal and kt >= TC * c else 0

                def values(u, kt):
                    c, g = units[u]
                    n = first_step[u] + kt
                    a = first_column(u, kt)
                    e.wait_ge(s.exp_done, 2 * n + 2)
                    if kt == 0 and u:
                        e.wait_ge(s.os_done, u)
                    for h in range(G):
                        w = VW * (G * g + h)
                        mm = e.matmul(O[32 * h:32 * h + 32, a:CH], t.V[:, kt, w:w + 32], Pb[:, n % 2, h, a:CH],
                                      start=(kt == 0), stop=(kt == tiles_of(c) - 1), skip_group_check=True)
                    mm.then_inc(s.pv_done, 1)

                for k, x in enumerate(max_blocks(0)):
                    max_block(0, k, *x)
                max_rows(0)
                for u, k, x in start:
                    max_block(u, k, *x)
                for u, (c, g) in enumerate(units):
                    e.wait_ge(mrow_stored[u % 2], 32 * (u // 2 + 1))
                    for kt in range(tiles_of(c)):
                        n = first_step[u] + kt
                        a = first_column(u, kt)
                        diagonal = causal and kt >= TC * c
                        for p in range(2):
                            if n:
                                e.wait_ge(s.exp_done, 2 * n - 1 + p)
                            for h in (2 * p, 2 * p + 1):
                                head = G * g + h
                                if diagonal:
                                    e.matmul(ps[:, h, a:a + P], t.identb[:, :], t.mask_kq[:, :], start=True,
                                             stop=False, skip_group_check=True)
                                mm = e.matmul(ps[:, h, a:CH], KS[:, head, kt * P:(kt + 1) * P],
                                              QS[:, c, head, a:CH], start=not diagonal, stop=True,
                                              skip_group_check=diagonal)
                            mm.then_inc(s.st_ready, 1)
                            for v, k, x in quarter(n, p):
                                max_block(v, k, *x)
                        if kt:
                            values(u, kt - 1)
                        for i in (2, 3):
                            for v, k, x in quarter(n, i):
                                max_block(v, k, *x)
                        if n - 1 in completes:
                            max_rows(completes[n - 1])
                        if u and kt == 1:
                            out_rows(u - 1)
                        if u and kt == 2 and g == 0:
                            chunk_columns(c - 1)
                        if u and kt == 3 and g == 0:
                            chunk_project(c - 1)
                    values(u, tiles_of(c) - 1)
                out_rows(len(units) - 1)
                chunk_columns(NC - 1)
                chunk_project(NC - 1)

            @block.scalar
            def _(e):
                for u, (c, g) in enumerate(units):
                    for kt in range(tiles_of(c)):
                        n = first_step[u] + kt
                        a = P * (kt - TC * c) if causal and kt >= TC * c else 0
                        for p in range(2):
                            e.wait_ge(s.st_ready, 2 * n + p + 1)
                            if n >= 2:
                                e.wait_ge(s.pv_done, n - 1)
                            e.activation(Pb[:, n % 2, 2 * p:2 * p + 2, a:CH], ps[:, 2 * p:2 * p + 2, a:CH], ACT.Exp)\
                                .then_inc(s.exp_done, 1)
                    e.wait_ge(s.pv_done, first_step[u + 1])
                    if u >= 2:
                        e.wait_ge(s.onorm, u - 1)
                    e.copy(OS[:, u % 2, :], O).then_inc(s.os_done, 1)

            @block.vector
            def _(e):
                e.memset(KS[:, :, :].rearrange("p h n -> p (h n)").bitcast(F32), ONES).then_inc(s.fill, 1)
                misc = 0
                rcps = 0

                def reduce_block(u, k, qt, h, b, width, masked):
                    n = first_max[u] + k
                    e.wait_ge(s.scored, n + 1)
                    e.tensor_reduce(part[:, u % 2, h * TC + qt, b:b + 1], ps[:, 4 + n % 2, 0:width], AX.X, ALU.max)\
                        .then_inc(s.reduced, 1)

                def unit_maxima(u):
                    e.wait_ge(s.reduced, first_max[u + 1])
                    if u >= 2:
                        e.wait_ge(mrow_stored[u % 2], 32 * (u // 2))
                    e.tensor_reduce(nmax[:, u % 2, :], part[:, u % 2, :, 0:blocks_of(units[u][0])], AX.X, ALU.max,
                                    negate=True).then_inc(s.nmax, 1)

                def max_rows(u):
                    nonlocal misc
                    e.wait_ge(s.misc_ready, misc + 1)
                    if u >= 2:
                        e.wait_ge(mrow_stored[u % 2], 32 * (u // 2))
                    e.tensor_copy(mrow[:, u % 2, 0, :], MISC[0:G * TC, 0:P]).then_inc(s.split, 1)
                    e.wait_ge(s.split, 2 * u + 1)
                    e.tensor_tensor(mrow[:, u % 2, 1, :], MISC[0:G * TC, 0:P], mrow[:, u % 2, 0, :], ALU.subtract)\
                        .then_inc(s.split, 1)
                    e.wait_ge(s.split, 2 * u + 2)
                    e.engine_nop().then_inc(s.misc_used, 1)
                    misc += 1

                def out_rows(u):
                    nonlocal misc, rcps
                    c, g = units[u]
                    e.wait_ge(s.misc_ready, misc + 1)
                    m = MISC.rearrange("p (q h w) -> p q h w", q=TC, h=G)
                    e.reciprocal(rcp[:, u % 2, :].rearrange("p (q h) -> p q h", q=TC), m[:, :, :, HD]).then_inc(s.rcp, 1)
                    e.wait_ge(s.rcp, u + 1)
                    if g == 0 and c >= 2:
                        e.wait_ge(s.oT, 2 * (c - 1))
                    e.tensor_tensor(o_tok[:, c % 2, :, G * HD * g:G * HD * (g + 1)].rearrange("p q (h d) -> p q h d", h=G),
                                    m[:, :, :, 0:HD],
                                    rcp[:, u % 2, :].rearrange("p (q h) -> p q h", q=TC).unsqueeze(3)
                                    .to_broadcast([P, TC, G, HD]), ALU.mult).then_inc(s.onorm, 1)
                    e.wait_ge(s.onorm, u + 1)
                    e.engine_nop().then_inc(s.misc_used, 1)
                    misc += 1

                def chunk_columns(c):
                    nonlocal misc
                    e.wait_ge(s.misc_ready, misc + 1)
                    e.tensor_copy(oT[:, c % 2, :], MISC).then_inc(s.misc_used, 1)
                    misc += 1

                def chunk_project(c):
                    nonlocal misc
                    e.wait_ge(s.misc_ready, misc + 1)
                    e.tensor_tensor(t.x[:, TC * c:TC * (c + 1), :], t.x[:, TC * c:TC * (c + 1), :],
                                    MISC.rearrange("p (q n) -> p q n", q=TC), ALU.add).then_inc(s.oT, 2)
                    e.wait_ge(s.oT, 2 * (c + 1))
                    e.engine_nop().then_inc(s.misc_used, 1)
                    misc += 1

                for k, x in enumerate(max_blocks(0)):
                    reduce_block(0, k, *x)
                unit_maxima(0)
                max_rows(0)
                for u, k, x in start:
                    reduce_block(u, k, *x)
                for u, (c, g) in enumerate(units):
                    for kt in range(tiles_of(c)):
                        n = first_step[u] + kt
                        for v, k, x in plan[n]:
                            reduce_block(v, k, *x)
                        if n - 1 in completes:
                            max_rows(completes[n - 1])
                        if n in completes:
                            unit_maxima(completes[n])
                        if u and kt == 1:
                            out_rows(u - 1)
                        if u and kt == 2 and g == 0:
                            chunk_columns(c - 1)
                        if u and kt == 3 and g == 0:
                            chunk_project(c - 1)
                out_rows(len(units) - 1)
                chunk_columns(NC - 1)
                chunk_project(NC - 1)


FI = 352
KT = -(-FI // P)
KL = FI - (KT - 1) * P
QB = 16
SCALE_MIN = 1e-12


def quantizer(e, t, link, chain):
    def quantize(out, src, magnitude, sign, n):
        nb = n // QB
        blocks = lambda a: a.rearrange("p (b k) -> p b k", k=QB)
        wide = lambda a: a.unsqueeze(2).to_broadcast([P, nb, QB])
        top, scale, inverse = t.q_top[:, 0:nb], t.q_scale[:, 0:nb], t.q_inverse[:, 0:nb]
        ratio, halves = t.q_ratio[:, 0:n], t.q_halves[:, 0:n]
        link(e.tensor_reduce(top, blocks(src), AX.X, ALU.max, apply_absolute_value=True), chain)
        link(e.tensor_scalar(scale, top, 1.0 / 6.0, SCALE_MIN, ALU.mult, ALU.max), chain)
        link(e.reciprocal(inverse, scale), chain)
        link(e.tensor_tensor(blocks(ratio), blocks(magnitude), wide(inverse), ALU.mult), chain)
        link(e.tensor_scalar(halves, ratio, 5.0, 2.0, ALU.is_gt, ALU.mult), chain)
        for mid in (3.5, 2.5):
            link(e.scalar_tensor_tensor(out=halves, in0=ratio, scalar=mid, in1=halves, op0=ALU.is_gt, op1=ALU.add), chain)
        link(e.tensor_scalar(halves, halves, 2.0, None, ALU.mult), chain)
        for mid in (1.75, 1.25, 0.75, 0.25):
            link(e.scalar_tensor_tensor(out=halves, in0=ratio, scalar=mid, in1=halves, op0=ALU.is_gt, op1=ALU.add), chain)
        link(e.scalar_tensor_tensor(out=halves, in0=halves, scalar=0.5, in1=sign, op0=ALU.mult, op1=ALU.mult), chain)
        return e.tensor_tensor(blocks(out), blocks(halves), wide(scale), ALU.mult)
    return quantize


def linker(e):
    counts = {}

    def link(ins, sem):
        counts[sem] = counts.get(sem, 0) + 1
        ins.then_inc(sem, 1)
        e.wait_ge(sem, counts[sem])
    return link


def fp4_feed_forward(nc, t, a):
    WN = 2 * KT * P + FI
    GT = 4
    GN = GT * FI
    with ExitStack() as ctx:
        s = semaphores(ctx, nc, "f0_", "ln_v ln_a load clear chain wq xq w_abs x_abs wT wT_ev xT xT_ev gate_up silu "
                       "hidden h_abs hq hT hT_ev down added")
        sb = lambda name, shape, dt=F32: ctx.enter_context(nc.sbuf_tensor("f0_" + name, shape, dt))
        xn = sb("xn", [P, NT, P])
        xq = sb("xq", [P, NT, P])
        xT = sb("xT", [P, N])
        w = sb("w", [P, WN])
        wT = sb("wT", [P, 2, KT * P])
        dT = sb("dT", [P, KT, P])
        magnitude = sb("magnitude", [P, N])
        sign = sb("sign", [P, N])
        silu = sb("silu", [P, 2, FI])
        hidden = sb("hidden", [P, 2, GN])
        hT = sb("hT", [P, 2, KT * P])
        t.q_ratio, t.q_halves = sb("ratio", [P, N]), sb("halves", [P, N])
        t.q_top, t.q_scale, t.q_inverse = sb("top", [P, N // QB]), sb("scale", [P, N // QB]), sb("inverse", [P, N // QB])
        ps = t.ps
        flat = lambda ap: ap.rearrange("p b n -> p (b n)")
        rows = lambda k: P if k < KT - 1 else KL
        ln_vector, ln_scalar = layer_norm(nc, t, t.x[:, :, :], xn[:, :, :], xq[:, :, :], s, NT)

        with nc.Block() as block:
            @block.sync
            def _(e):
                e.wait_ge(s.clear, 1)
                for i, name in enumerate(("L0_ffn_w_gate", "L0_ffn_w_up")):
                    v = w[:, i * KT * P:(i + 1) * KT * P].rearrange("p (k n) -> p k n", n=P)
                    e.dma_start(v[:, 0:KT - 1, :], a[name][0:(KT - 1) * P, :].rearrange("(k p) n -> p k n", p=P))\
                        .then_inc(s.load, 16)
                    e.dma_start(v[0:KL, KT - 1, :], a[name][(KT - 1) * P:FI, :]).then_inc(s.load, 16)
                e.dma_start(w[:, 2 * KT * P:WN], a["L0_ffn_w_down"]).then_inc(s.load, 16)

            @block.gpsimd
            def _(e):
                e.memset(w[:, :], 0.0).then_inc(s.clear, 1)

            @block.tensor
            def _(e):
                e.wait_ge(s.wq, 1)
                for i in range(2):
                    for k in range(KT):
                        e.transpose(ps[:, i, k * P:(k + 1) * P], w[:, (i * KT + k) * P:(i * KT + k + 1) * P],
                                    t.ident[:, :]).then_inc(s.wT, 1)
                for k in range(KT):
                    at = 2 * KT * P + k * P
                    e.transpose(ps[0:rows(k), 2, k * P:(k + 1) * P], w[:, at:at + rows(k)], t.ident[:, :])\
                        .then_inc(s.wT, 1)
                e.wait_ge(s.xq, 1)
                for i in range(NT):
                    e.transpose(ps[:, 4 + i // TC, (i % TC) * P:(i % TC + 1) * P], xq[:, i, :], t.ident[:, :])\
                        .then_inc(s.xT, 1)
                e.wait_ge(s.wT_ev, 4)
                e.wait_ge(s.xT_ev, 1)

                def gate_up(i):
                    if i >= 2:
                        e.wait_ge(s.hidden, i - 1)
                    for j in range(2):
                        mm = e.matmul(ps[:, 2 * (i % 2) + j, 0:FI], xT[:, i * P:(i + 1) * P], wT[:, j, 0:FI],
                                      start=True, stop=True)
                    mm.then_inc(s.gate_up, 1)

                def down(i):
                    g = i // GT
                    e.wait_ge(s.hq, g + 1)
                    if i >= 2:
                        e.wait_ge(s.hT_ev, i - 1)
                    for k in range(KT):
                        at = (i % GT) * FI + k * P
                        tr = e.transpose(ps[0:rows(k), 4 + i % 2, k * P:(k + 1) * P], hidden[:, g % 2, at:at + rows(k)],
                                         t.ident[:, :])
                    tr.then_inc(s.hT, 1)

                def down_product(i):
                    g = i // GT
                    e.wait_ge(s.hT_ev, i + 1)
                    if g >= 2:
                        e.wait_ge(s.added, g - 1)
                    for k in range(KT):
                        mm = e.matmul(ps[:, 6 + g % 2, (i % GT) * P:(i % GT + 1) * P], hT[0:rows(k), i % 2, k * P:(k + 1) * P],
                                      dT[0:rows(k), k, :], start=(k == 0), stop=(k == KT - 1))
                    mm.then_inc(s.down, 1)

                for g in range(NT // GT + 1):
                    if g < NT // GT:
                        for i in range(GT * g, GT * g + GT):
                            gate_up(i)
                    if g:
                        for i in range(GT * (g - 1), GT * g):
                            down(i)
                            if i > GT * (g - 1):
                                down_product(i - 1)
                        down_product(GT * g - 1)

            @block.vector
            def _(e):
                link = linker(e)
                quantize = quantizer(e, t, link, s.chain)
                e.wait_ge(s.load, 80)
                e.wait_ge(s.w_abs, 2)
                link(quantize(w[:, :], w[:, :], magnitude[:, 0:WN], sign[:, 0:WN], WN), s.wq)
                ln_vector(e)
                e.wait_ge(s.ln_v, 7)
                e.wait_ge(s.x_abs, 2)
                link(quantize(flat(xq[:, :, :]), flat(xn[:, :, :]), magnitude[:, :], sign[:, :], N), s.xq)
                e.wait_ge(s.xT, NT)
                e.tensor_copy(xT[:, :], flat(ps[:, 4:8, :])).then_inc(s.xT_ev, 1)

                def add_group(g):
                    e.wait_ge(s.down, GT * (g + 1))
                    e.tensor_tensor(t.x[:, GT * g:GT * (g + 1), :], t.x[:, GT * g:GT * (g + 1), :],
                                    ps[:, 6 + g % 2, :].rearrange("p (q n) -> p q n", q=GT), ALU.add).then_inc(s.added, 1)

                for g in range(NT // GT):
                    if g >= 2:
                        e.wait_ge(s.hT, GT * (g - 1))
                    for i in range(GT * g, GT * g + GT):
                        e.wait_ge(s.silu, i + 1)
                        e.tensor_tensor(hidden[:, g % 2, (i % GT) * FI:(i % GT + 1) * FI], silu[:, i % 2, :],
                                        ps[:, 2 * (i % 2) + 1, 0:FI], ALU.mult).then_inc(s.hidden, 1)
                    e.wait_ge(s.hidden, GT * (g + 1))
                    e.wait_ge(s.h_abs, 2 * (g + 1))
                    link(quantize(hidden[:, g % 2, :], hidden[:, g % 2, :], magnitude[:, 0:GN], sign[:, 0:GN], GN), s.hq)
                    if g:
                        add_group(g - 1)
                add_group(NT // GT - 1)
                e.wait_ge(s.added, NT // GT)

            @block.scalar
            def _(e):
                e.wait_ge(s.load, 80)
                e.activation(magnitude[:, 0:WN], w[:, :], ACT.Abs).then_inc(s.w_abs, 1)
                e.activation(sign[:, 0:WN], w[:, :], ACT.Sign).then_inc(s.w_abs, 1)
                ln_scalar(e)
                e.wait_ge(s.wT, 3 * KT)
                for i in range(2):
                    e.copy(wT[:, i, :], ps[:, i, 0:KT * P]).then_inc(s.wT_ev, 1)
                e.copy(dT[:, 0:KT - 1, :], ps[:, 2, 0:(KT - 1) * P].rearrange("p (k n) -> p k n", n=P)).then_inc(s.wT_ev, 1)
                e.copy(dT[0:KL, KT - 1, :], ps[0:KL, 2, (KT - 1) * P:KT * P]).then_inc(s.wT_ev, 1)
                e.wait_ge(s.ln_v, 7)
                e.activation(magnitude[:, :], flat(xn[:, :, :]), ACT.Abs).then_inc(s.x_abs, 1)
                e.activation(sign[:, :], flat(xn[:, :, :]), ACT.Sign).then_inc(s.x_abs, 1)

                def transposed(i):
                    e.wait_ge(s.hT, i + 1)
                    if i >= 2:
                        e.wait_ge(s.down, i - 1)
                    e.copy(hT[:, i % 2, 0:(KT - 1) * P], ps[:, 4 + i % 2, 0:(KT - 1) * P])
                    e.copy(hT[0:KL, i % 2, (KT - 1) * P:KT * P], ps[0:KL, 4 + i % 2, (KT - 1) * P:KT * P])\
                        .then_inc(s.hT_ev, 1)

                for g in range(NT // GT + 1):
                    if g < NT // GT:
                        for i in range(GT * g, GT * g + GT):
                            e.wait_ge(s.gate_up, i + 1)
                            if i >= 2:
                                e.wait_ge(s.hidden, i - 1)
                            e.activation(silu[:, i % 2, :], ps[:, 2 * (i % 2), 0:FI], ACT.Silu).then_inc(s.silu, 1)
                        e.wait_ge(s.hidden, GT * (g + 1))
                        if g:
                            e.wait_ge(s.hq, g)
                        else:
                            e.wait_ge(s.xq, 1)
                        e.activation(magnitude[:, 0:GN], hidden[:, g % 2, :], ACT.Abs).then_inc(s.h_abs, 1)
                        e.activation(sign[:, 0:GN], hidden[:, g % 2, :], ACT.Sign).then_inc(s.h_abs, 1)
                    if g:
                        for i in range(GT * (g - 1), GT * g):
                            transposed(i)


DEPTH = 6
WIN = 32
LD = 64
LH = 16
INNER = LH * LD
PAIRS = LH // 2
ROT = LD // 2
QG = 4
LG = LH // QG
VL = LD + 1
MI = 341
MT = -(-MI // P)
ML = MI - (MT - 1) * P
QK_SCALE = 8.0
LN_RANGE = 2.0 ** 24
LN_TINY = 2.0 ** -60
NORM_MIN = 1e-12
START = 1


TURNS = [(0, r) for r in range(4)]
DRAINS = []
for _T in range(NT):
    DRAINS += [(_T, 0), (_T, 1), (_T, 2)]
    if _T:
        TURNS += [(_T - 1, 4), (_T - 1, 5)]
        DRAINS += [(_T - 1, 3)]
    if _T + 1 < NT:
        TURNS += [(_T + 1, r) for r in range(4)]
TURNS += [(NT - 1, 4), (NT - 1, 5)]
DRAINS += [(NT - 1, 3)]


def turn_index(T, r):
    return TURNS.index((T, r))


def d_index(T, r):
    return DRAINS.index((T, r))


def shift_tokens(e, XS, X, signal):
    e.tensor_copy(XS[0:P // 2, :], X[0:P // 2, :]).then_inc(signal, 1)
    e.tensor_copy(XS[P // 2:P, 1:N], X[P // 2:P, 0:N - 1]).then_inc(signal, 1)


LN_EXP = "natural_log_exp_and_others"
VAR_BANK = [0, 1, 2, 7]
SHIFTS = 2 + 2 * NC


def layers(nc, t, a):
    with ExitStack() as ctx:
        s = semaphores(ctx, nc, "l_", "w_qkv w_tab w_o w_mlp xs tab a_ready square total root qn cosine v_done rotated "
                       "t_ready t_free d_ready d_free split mrow_even mrow_odd prev_ready prev_done st_ready exp_done pv_done normed "
                       "mean centred varied ln_sq rstd xn gate gelu up hidden y half log bound rcp summed")
        sb = lambda name, shape, dt=F32: ctx.enter_context(nc.sbuf_tensor("l_" + name, shape, dt))
        X, ps = t.X, t.ps
        XS = sb("XS", [P, N])
        w_qkv = sb("w_qkv", [P, 3 * INNER])
        w_o = sb("w_o", [P, PAIRS, P])
        w_1 = sb("w_1", [P, 2 * MI])
        w_2 = sb("w_2", [P, MT, P])
        b_1 = sb("b_1", [P, 2, MT])
        vec = sb("vec", [P, 3])
        scales = sb("scales", [P, 4, LD])
        base = sb("base", [P, 4, NT, LD])
        tab = sb("tab", [P, 4, NT, LD])
        square = sb("square", [P, LH, LD])
        norm = sb("norm", [P, 4, LH])
        qn = sb("qn", [P, 2, LH, LD])
        cosine = sb("cosine", [P, 2, LH, LD])
        sine = sb("sine", [P, LH, LD])
        hat = sb("hat", [P, 2, LH * LD])
        qT = sb("qT", [P, 2, PAIRS, 2, P])
        qTb = sb("qTb", [P, 2, PAIRS, 2 * P], BF16)
        kT = sb("kT", [P, 2, PAIRS, WIN + P])
        kTb = sb("kTb", [P, 2, PAIRS, WIN + P], BF16)
        V = sb("V", [P, 3, LH, VL])
        nmax = sb("nmax", [P, LH])
        msplit = sb("msplit", [LH, 2, 2, P], BF16)
        mrow = sb("mrow", [2, 2, LH * P], BF16)
        weights = sb("weights", [P, 2, QG * P])
        before = sb("before", [P, LH * WIN])
        rcp = sb("rcp", [P, QG])
        o_tok = sb("o_tok", [P, 2, LH, LD])
        oT = sb("oT", [P, PAIRS, P])
        xn = sb("xn", [P, N])
        gelu = sb("gelu", [P, MT, CH])
        mask_c = sb("mask_c", [P, 2, CH], BF16)
        mask_d = sb("mask_d", [P, CH], BF16)
        mask_p = sb("mask_p", [P, CH], BF16)
        ones2 = sb("ones2", [2, P], BF16)
        means = sb("means", [P, P])
        const = sb("const", [P, 4])
        mrow_stored = [s.mrow_even, s.mrow_odd]
        flat2 = lambda ap: ap.rearrange("p b n -> p (b n)")
        rows = lambda k: P if k < MT - 1 else ML
        tiles = lambda ap: ap.rearrange("p (i n) -> p i n", i=NT)
        hidden = o_tok[:, :, :, :].rearrange("p i h d -> p (i h d)")[:, 0:MT * CH].rearrange("p (k n) -> p k n", k=MT)
        ln_square = qn[:, :, :, :].rearrange("p i h d -> p (i h d)")
        ln_rstd = cosine[:, :, :, :].rearrange("p i h d -> p (i h d)")

        with ExitStack() as c0:
            s0 = semaphores(c0, nc, "l0_", "load xT x clear ln_v ln_a")
            ln_vector, ln_scalar = layer_norm(nc, t, t.x[:, :, :], tiles(xn[:, :]), tiles(ln_square), s0, NT)
            with nc.Block() as block:
                @block.sync
                def _(e):
                    for dst, name in ((base[:, :, :, :], "c_base"), (mask_c[:, :, :], "c_mask_c"), (mask_d[:, :], "c_mask_d"),
                                      (mask_p[:, :], "c_mask_p"), (const[:, :], "c_const")):
                        e.dma_start(dst, a[name]).then_inc(s0.load, 16)
                    e.wait_ge(s0.load, 80)

                @block.gpsimd
                def _(e):
                    e.memset(XS[:, :], 0.0).then_inc(s0.clear, 1)
                    e.memset(qT[:, :, :, :, :], 0.0)
                    e.memset(qTb[:, :, :, :], 0.0)
                    e.memset(kT[:, :, :, :], 0.0)
                    e.memset(kTb[:, :, :, :], 0.0)
                    e.memset(V[:, :, :, :], 1.0)
                    e.memset(ones2[:, :], 1.0)
                    e.memset(means[:, :], 1.0 / P)

                @block.tensor
                def _(e):
                    e.wait_ge(s0.ln_v, 7)
                    for i in range(NT):
                        e.transpose(ps[:, i // TC, (i % TC) * P:(i % TC + 1) * P], tiles(xn[:, :])[:, i, :], t.ident[:, :])\
                            .then_inc(s0.xT, 1)

                @block.scalar
                def _(e):
                    ln_scalar(e)

                @block.vector
                def _(e):
                    ln_vector(e)
                    e.wait_ge(s0.xT, NT)
                    e.tensor_copy(X[:, :], flat2(ps[:, 0:4, :])).then_inc(s0.x, 1)
                    e.wait_ge(s0.x, 1)
                    e.wait_ge(s0.clear, 1)
                    shift_tokens(e, XS, X, s0.x)

        with nc.Block() as block:
            @block.sync
            def _(e):
                e.sem_inc(s.mrow_even, START)
                e.sem_inc(s.mrow_odd, START)

                def load_weights(l):
                    e.wait_ge(s.a_ready, START + l * (3 * NT))
                    e.dma_start(w_qkv[:, :], a["L1_ffn_Wqkv"][l]).then_inc(s.w_qkv, 16)
                    e.wait_ge(s.tab, START + l * 4)
                    for i, name in enumerate(("L1_ffn_q_scale", "L1_ffn_k_scale")):
                        v = a[name][l].rearrange("(o d) -> o d", o=1)
                        e.dma_start(scales[:, 2 * i, :], v.partition_broadcast(P)).then_inc(s.w_tab, 16)
                        e.dma_start(scales[:, 2 * i + 1, 0:ROT], v[:, ROT:LD].partition_broadcast(P)).then_inc(s.w_tab, 16)
                        e.dma_start(scales[:, 2 * i + 1, ROT:LD], v[:, 0:ROT].partition_broadcast(P)).then_inc(s.w_tab, 16)
                    e.wait_ge(s.d_ready, START + l * (4 * NT))
                    e.dma_start(w_o[:, :, :], a["L1_ffn_Wo"][l].rearrange("(j p) n -> p j n", p=P)).then_inc(s.w_o, 16)

                def load_forward(l):
                    e.wait_ge(s.xs, START + l * SHIFTS)
                    e.dma_start(w_1[:, :], a["L1_ffn_W1"][l]).then_inc(s.w_mlp, 16)
                    w2 = a["L1_ffn_W2"][l]
                    full = (MT - 1) * P
                    e.dma_start(w_2[:, 0:MT - 1, :], w2[0:full, :].rearrange("(k p) n -> p k n", p=P)).then_inc(s.w_mlp, 16)
                    e.dma_start(w_2[0:ML, MT - 1, :], w2[full:MI, :]).then_inc(s.w_mlp, 16)
                    for i in range(2):
                        b1 = a["L1_ffn_b1"][l, i * MI:(i + 1) * MI]
                        for k in range(MT):
                            e.dma_start(b_1[0:rows(k), i, k:k + 1], b1[k * P:k * P + rows(k)].rearrange("(p o) -> p o", o=1))\
                                .then_inc(s.w_mlp, 16)
                    for i, name in enumerate(("L1_ffn_ln_g", "L1_ffn_ln_b", "L1_ffn_b2")):
                        e.dma_start(vec[:, i:i + 1], a[name][l].rearrange("(p o) -> p o", o=1)).then_inc(s.w_mlp, 16)

                def store_maxima(l):
                    for T in range(NT):
                        if T == 2:
                            load_forward(l)
                        e.wait_ge(s.d_free, START + l * (4 * NT) + d_index(T, 2) + 1)
                        for j in range(2):
                            e.dma_start(mrow[j:j + 1, T % 2, :], msplit[:, T % 2, j, :]).then_inc(mrow_stored[T % 2], 16)

                load_weights(0)
                if DEPTH > 1:
                    with e.Fori(0, DEPTH - 1) as l:
                        store_maxima(l)
                        load_weights(l + 1)
                store_maxima(DEPTH - 1)

            @block.gpsimd
            def _(e):
                e.sem_inc(s.tab, START)
                e.sem_inc(s.rotated, START)

                def rotate(l, T, i):
                    n = (l * NT + T) * 2 + i
                    e.wait_ge(s.qn, n + 1)
                    swap = qn[:, i, :, :]
                    table = tab[:, 2 * i + 1, T, :].unsqueeze(1).to_broadcast([P, LH, LD])
                    e.wait_ge(s.rotated, START + n * 3)
                    e.tensor_tensor(sine[:, :, 0:ROT], swap[:, :, ROT:LD], table[:, :, 0:ROT], ALU.mult).then_inc(s.rotated, 1)
                    e.tensor_tensor(sine[:, :, ROT:LD], swap[:, :, 0:ROT], table[:, :, ROT:LD], ALU.mult).then_inc(s.rotated, 1)
                    e.wait_ge(s.rotated, START + n * 3 + 2)
                    e.wait_ge(s.cosine, START + n + 1)
                    e.tensor_tensor(hat[:, i, :].rearrange("p (h d) -> p h d", h=LH), cosine[:, i, :, :], sine[:, :, :], ALU.add)\
                        .then_inc(s.rotated, 1)

                def begin(l):
                    e.wait_ge(s.w_tab, (l + 1) * 96)
                    e.wait_ge(s.cosine, START + l * (2 * NT))
                    e.wait_ge(s.rotated, START + l * (6 * NT))
                    for i in range(4):
                        e.tensor_tensor(tab[:, i, :, :], base[:, i, :, :],
                                        scales[:, i, :].unsqueeze(1).to_broadcast([P, NT, LD]), ALU.mult).then_inc(s.tab, 1)
                    e.wait_ge(s.tab, START + (l + 1) * 4)
                    for i in range(2):
                        rotate(l, 0, i)

                def tiles_after(l):
                    for T in range(1, NT):
                        for i in range(2):
                            rotate(l, T, i)

                begin(0)
                with e.Fori(0, DEPTH - 1) as l:
                    tiles_after(l)
                    begin(l + 1)
                tiles_after(DEPTH - 1)

            @block.tensor
            def _(e):
                e.sem_inc(s.pv_done, START + 1)
                e.sem_inc(s.a_ready, START)
                e.sem_inc(s.d_ready, START)

                def project(l, T, i):
                    n = l * NT + T
                    if i == 0:
                        e.wait_ge(s.v_done, START + n)
                    else:
                        e.wait_ge(s.qn, 2 * n + i)
                    for b in range(2):
                        at = i * INNER + b * CH
                        mm = e.matmul(ps[:, b, :], XS[:, T * P:(T + 1) * P], w_qkv[:, at:at + CH], start=True, stop=True)
                    mm.then_inc(s.a_ready, 1)

                def turn_qk(l, T, r):
                    i = r // 2
                    e.wait_ge(s.rotated, START + ((l * NT + T) * 2 + i) * 3 + 3)
                    turn_at(l, T, r, lambda j: hat[:, i, (4 * (r % 2) + j) * P:(4 * (r % 2) + j + 1) * P])

                def turn_at(l, T, r, source):
                    n = l * (6 * NT) + turn_index(T, r)
                    e.wait_ge(s.t_free, START + n)
                    for j in range(4):
                        tr = e.transpose(ps[:, 2, j * P:(j + 1) * P], source(j), t.ident[:, :])
                    tr.then_inc(s.t_ready, 1)

                def turn_o(l, T, r):
                    e.wait_ge(s.normed, START + (l * NT + T + 1) * LG)
                    flat = o_tok[:, T % 2, :, :].rearrange("p h d -> p (h d)")
                    turn_at(l, T, r, lambda j: flat[:, (4 * (r - 4) + j) * P:(4 * (r - 4) + j + 1) * P])

                def compact(l, T, r):
                    n = l * (4 * NT) + d_index(T, r)
                    if r == 0:
                        e.wait_ge(s.d_free, START + n)
                    e.wait_ge(s.half, (l * NT + T) * 4 + r + 3)
                    e.matmul(ps[:, 4 - r, :], t.identb[:, :], mask_c[:, 0 if T else 1, :], start=True, stop=False,
                             skip_group_check=True)
                    for k in range(4):
                        for w in range(4):
                            half = LD * (w % 2)
                            at = LD * (2 * k + w // 2)
                            mm = e.matmul(ps[half:half + LD, 4 - r, at:at + LD], qTb[:, T % 2, 4 * r + k, LD * w:LD * (w + 1)],
                                          kTb[:, T % 2, 4 * r + k, WIN * w:WIN * (w + 2)],
                                          start=False, stop=True, skip_group_check=True)
                    mm.then_inc(s.d_ready, 1)

                def max_rows(l, T):
                    e.wait_ge(s.d_free, START + l * (4 * NT) + d_index(T, 2))
                    e.transpose(ps[0:LH, 4, 0:P], nmax[:, :], t.ident[:, :]).then_inc(s.d_ready, 1)

                def out_project(l, T):
                    e.wait_ge(s.t_free, START + l * (6 * NT) + turn_index(T, 5) + 1)
                    if T == 0:
                        e.wait_ge(s.w_o, (l + 1) * 16)
                    e.wait_ge(s.d_free, START + l * (4 * NT) + d_index(T, 3))
                    for j in range(PAIRS):
                        mm = e.matmul(ps[:, 4, 0:P], w_o[:, j, :], oT[:, j, :], start=(j == 0), stop=(j == PAIRS - 1))
                    mm.then_inc(s.d_ready, 1)

                def scores_before(l, T):
                    e.wait_ge(s.prev_done, START + l * (NT - 1) + T - 1)
                    out = ps[P - WIN:P, 3, :]
                    e.matmul(out, t.identb[:, P - WIN:P], mask_p[:, :], start=True, stop=False, skip_group_check=True)
                    e.matmul(out.rearrange("p (j q) -> p j q", j=PAIRS), ones2[:, 0:WIN],
                             mrow[:, T % 2, :].rearrange("p (j q) -> p j q", j=PAIRS)[:, :, 0:2 * WIN],
                             start=False, stop=False, skip_group_check=True)
                    for j in range(PAIRS):
                        mm = e.matmul(out[:, 2 * WIN * j:2 * WIN * (j + 1)], kT[:, T % 2, j, 0:WIN], qT[:, T % 2, j, :, 0:WIN],
                                      start=False, stop=True, skip_group_check=True)
                    mm.then_inc(s.prev_ready, 1)

                def scores(l, T, g):
                    n = (l * NT + T) * LG + g
                    e.wait_ge(s.exp_done, START + n)
                    bank = ps[:, 5 + g % 2, :]
                    e.matmul(bank, t.identb[:, :], mask_d[:, :], start=True, stop=False, skip_group_check=True)
                    rows2 = mrow[:, T % 2, :].rearrange("p (j w two q) -> p j two w q", j=PAIRS, two=2, q=WIN)
                    for k in range(QG // 2):
                        e.matmul(bank[:, 2 * P * k:2 * P * (k + 1)].rearrange("p (two w q) -> p two w q", two=2, q=WIN),
                                 ones2[:, :], rows2[:, g * (QG // 2) + k, :, :, :], start=False, stop=False, skip_group_check=True)
                    for k in range(QG // 2):
                        j = g * (QG // 2) + k
                        mm = e.matmul(bank[:, 2 * P * k:2 * P * (k + 1)], kT[:, T % 2, j, WIN:WIN + P], qT[:, T % 2, j, :, :],
                                      start=False, stop=True, skip_group_check=True)
                    mm.then_inc(s.st_ready, 1)

                def values(l, T, g):
                    n = (l * NT + T) * LG + g
                    e.wait_ge(s.exp_done, START + n + 2)
                    e.wait_ge(s.normed, START + n)
                    if T and g == 0:
                        e.wait_ge(s.prev_done, START + l * (NT - 1) + T)
                    for k in range(QG):
                        h = QG * g + k
                        mm = e.matmul(ps[:, 7, VL * k:VL * (k + 1)], weights[:, g % 2, P * k:P * (k + 1)], V[:, T % 3, h, :],
                                      start=True, stop=(T == 0), skip_group_check=True)
                        if T:
                            mm = e.matmul(ps[0:WIN, 7, VL * k:VL * (k + 1)], before[P - WIN:P, WIN * h:WIN * (h + 1)],
                                          V[P - WIN:P, (T - 1) % 3, h, :], start=False, stop=True, skip_group_check=True)
                    mm.then_inc(s.pv_done, 1)

                def attend(l):
                    e.wait_ge(s.xs, START + l * SHIFTS)
                    for r in range(2):
                        compact(l, 0, r)
                    for T in range(NT):
                        ahead = T + 1 < NT
                        if T:
                            turn_o(l, T - 1, 4)
                        if ahead:
                            project(l, T + 1, 0)
                        max_rows(l, T)
                        if T:
                            turn_o(l, T - 1, 5)
                            out_project(l, T - 1)
                        e.wait_ge(mrow_stored[T % 2], START + (l * (NT // 2) + T // 2 + 1) * 32)
                        e.wait_ge(s.v_done, START + l * NT + T + 1)
                        if T:
                            scores_before(l, T)
                        scores(l, T, 0)
                        if ahead:
                            project(l, T + 1, 1)
                        scores(l, T, 1)
                        values(l, T, 0)
                        if ahead:
                            turn_qk(l, T + 1, 0)
                        scores(l, T, 2)
                        values(l, T, 1)
                        if ahead:
                            project(l, T + 1, 2)
                            turn_qk(l, T + 1, 1)
                        scores(l, T, 3)
                        if ahead:
                            turn_qk(l, T + 1, 2)
                        values(l, T, 2)
                        if ahead:
                            turn_qk(l, T + 1, 3)
                        values(l, T, 3)
                        if ahead:
                            compact(l, T + 1, 0)
                            compact(l, T + 1, 1)
                    turn_o(l, NT - 1, 4)
                    turn_o(l, NT - 1, 5)
                    out_project(l, NT - 1)

                def gate_up(l, c, k):
                    n = l * NC + c
                    bank = 3 + 2 * ((c * MT + k) % 2)
                    if k == 0:
                        e.wait_ge(s.xn, 2 * n + 2)
                    if c * MT + k >= 2:
                        e.wait_ge(s.hidden, n * MT + k - 1)
                    else:
                        e.wait_ge(s.centred, (l + 1) * NC)
                    for to, at, signal in ((bank, MI, s.gate), (bank + 1, 0, s.up)):
                        e.matmul(ps[0:rows(k), to, :], w_1[:, at + k * P:at + k * P + rows(k)], xn[:, c * CH:(c + 1) * CH],
                                 start=True, stop=True).then_inc(signal, 1)

                def down(l, c):
                    n = l * NC + c
                    e.wait_ge(s.hidden, (n + 1) * MT)
                    if c:
                        e.wait_ge(s.summed, n)
                    else:
                        e.wait_ge(s.rstd, (l + 1) * NC)
                    for k in range(MT):
                        mm = e.matmul(ps[:, 7, :], w_2[0:rows(k), k, :], hidden[0:rows(k), k, :],
                                      start=(k == 0), stop=(k == MT - 1))
                    mm.then_inc(s.y, 1)

                def forward(l, following):
                    e.wait_ge(s.xs, START + l * SHIFTS + 2)
                    for c in range(NC):
                        e.matmul(ps[:, 3 + c, :], means[:, :], XS[:, c * CH:(c + 1) * CH], start=True, stop=True)\
                            .then_inc(s.mean, 1)
                    for c in range(NC):
                        e.wait_ge(s.ln_sq, l * NC + c + 1)
                        e.matmul(ps[:, VAR_BANK[c], :], means[:, :], ln_square[:, c * CH:(c + 1) * CH], start=True, stop=True)\
                            .then_inc(s.varied, 1)
                    e.wait_ge(s.w_mlp, (l + 1) * 192)
                    for c in range(NC):
                        gate_up(l, c, 0)
                        if c:
                            down(l, c - 1)
                        gate_up(l, c, 1)
                        if following and c == NC - 1:
                            project(l + 1, 0, 1)
                        gate_up(l, c, 2)
                        if following and c == NC - 2:
                            e.wait_ge(s.w_qkv, (l + 2) * 16)
                            e.wait_ge(s.xs, START + l * SHIFTS + 4)
                            project(l + 1, 0, 0)
                    down(l, NC - 1)
                    if following:
                        project(l + 1, 0, 2)
                        for r in range(4):
                            turn_qk(l + 1, 0, r)

                e.wait_ge(s.w_qkv, 16)
                for i in range(3):
                    project(0, 0, i)
                for r in range(4):
                    turn_qk(0, 0, r)
                with e.Fori(0, DEPTH - 1) as l:
                    attend(l)
                    forward(l, True)
                attend(DEPTH - 1)
                forward(DEPTH - 1, False)

            @block.scalar
            def _(e):
                e.sem_inc(s.exp_done, START + 1)
                e.sem_inc(s.v_done, START)
                e.sem_inc(s.t_free, START)
                e.sem_inc(s.prev_done, START)

                def squares(l, T, i):
                    n = (l * NT + T) * 2 + i
                    e.wait_ge(s.a_ready, START + (l * NT + T) * 3 + i + 1)
                    e.wait_ge(s.total, START + n)
                    e.activation(square[:, :, :].rearrange("p h d -> p (h d)"), flat2(ps[:, 0:2, :]), ACT.Square)\
                        .then_inc(s.square, 1)

                def inverse_norms(l, T, i):
                    n = (l * NT + T) * 2 + i
                    e.wait_ge(s.total, START + n + 1)
                    e.activation(norm[:, 1, :], norm[:, 0, :], ACT.Ln, bias=const[:, 0:1], scale=LN_RANGE).then_inc(s.root, 1)
                    e.wait_ge(s.root, 2 * n + 1)
                    e.activation(norm[:, 2, :], norm[:, 1, :], ACT.Exp, bias=const[:, 1:2], scale=-0.5).then_inc(s.root, 1)

                def store_values(l, T):
                    e.wait_ge(s.a_ready, START + (l * NT + T) * 3 + 3)
                    e.copy(V[:, T % 3, :, 0:LD], flat2(ps[:, 0:2, :]).rearrange("p (h d) -> p h d", h=LH))\
                        .then_inc(s.v_done, 1)

                def store_qk(l, T, r):
                    n = l * (6 * NT) + turn_index(T, r)
                    e.wait_ge(s.t_ready, n + 1)
                    j0 = 4 * (r % 2)
                    if r < 2:
                        bank = ps[:, 2, :].rearrange("p (j q) -> p j q", j=4)
                        e.copy(qT[0:LD, T % 2, j0:j0 + 4, 0, :], bank[0:LD, :, :])
                        e.copy(qT[LD:P, T % 2, j0:j0 + 4, 1, :], bank[LD:P, :, :]).then_inc(s.t_free, 1)
                    else:
                        e.copy(kT[:, T % 2, j0:j0 + 4, WIN:WIN + P], ps[:, 2, :].rearrange("p (j n) -> p j n", j=4))\
                            .then_inc(s.t_free, 1)
                    if r == 3 and T + 1 < NT:
                        e.wait_ge(s.t_free, START + n + 1)
                        e.activation(kT[:, (T + 1) % 2, :, 0:WIN], kT[:, T % 2, :, P:P + WIN], ACT.Copy,
                                     scale=const[:, 3:4] if (T + 1) % TC == 0 else 1.0)

                def store_o(l, T, r):
                    n = l * (6 * NT) + turn_index(T, r)
                    e.wait_ge(s.t_ready, n + 1)
                    j0 = 4 * (r - 4)
                    e.copy(oT[:, j0:j0 + 4, :].rearrange("p j n -> p (j n)"), ps[:, 2, :]).then_inc(s.t_free, 1)

                def exp(l, T, g):
                    n = (l * NT + T) * LG + g
                    e.wait_ge(s.st_ready, n + 1)
                    e.wait_ge(s.pv_done, START + n)
                    e.activation(weights[:, g % 2, :], ps[:, 5 + g % 2, :], ACT.Exp).then_inc(s.exp_done, 1)

                def attend(l):
                    for T in range(NT):
                        ahead = T + 1 < NT
                        if T:
                            store_o(l, T - 1, 4)
                        if ahead:
                            squares(l, T + 1, 0)
                        if T:
                            store_o(l, T - 1, 5)
                        if ahead:
                            inverse_norms(l, T + 1, 0)
                        if T:
                            e.wait_ge(s.prev_ready, l * (NT - 1) + T)
                            e.wait_ge(s.pv_done, START + (l * NT + T) * LG + 1)
                            e.activation(before[P - WIN:P, :], ps[P - WIN:P, 3, :], ACT.Exp).then_inc(s.prev_done, 1)
                        exp(l, T, 0)
                        if ahead:
                            squares(l, T + 1, 1)
                        exp(l, T, 1)
                        if ahead:
                            inverse_norms(l, T + 1, 1)
                            store_qk(l, T + 1, 0)
                        exp(l, T, 2)
                        if ahead:
                            store_values(l, T + 1)
                            store_qk(l, T + 1, 1)
                        exp(l, T, 3)
                        if ahead:
                            store_qk(l, T + 1, 2)
                            store_qk(l, T + 1, 3)
                    store_o(l, NT - 1, 4)
                    store_o(l, NT - 1, 5)

                def gelu_of(l, c, k):
                    n = l * NC + c
                    e.wait_ge(s.gate, n * MT + k + 1)
                    if c:
                        e.wait_ge(s.hidden, (n - 1) * MT + k + 1)
                    e.activation(gelu[0:rows(k), k, :], ps[0:rows(k), 3 + 2 * ((c * MT + k) % 2), :], ACT.Gelu,
                                 bias=b_1[0:rows(k), 1, k:k + 1]).then_inc(s.gelu, 1)

                def forward(l, following):
                    for c in range(NC):
                        cols = slice(c * CH, (c + 1) * CH)
                        e.wait_ge(s.centred, l * NC + c + 1)
                        e.activation(ln_square[:, cols], xn[:, cols], ACT.Square).then_inc(s.ln_sq, 1)
                    for c in range(NC):
                        cols = slice(c * CH, (c + 1) * CH)
                        e.wait_ge(s.varied, l * NC + c + 1)
                        e.activation(ln_rstd[:, cols], ps[:, VAR_BANK[c], :], ACT.Ln, bias=const[:, 2:3]).then_inc(s.log, 1)
                        e.wait_ge(s.log, l * NC + c + 1)
                        e.activation(ln_rstd[:, cols], ln_rstd[:, cols], ACT.Exp, scale=-0.5).then_inc(s.rstd, 1)
                    for c in range(NC):
                        for k in range(MT):
                            gelu_of(l, c, k)
                        if following and c >= NC - 2:
                            e.preload_act_table_set(LN_EXP)
                            squares(l + 1, 0, c - (NC - 2))
                            inverse_norms(l + 1, 0, c - (NC - 2))
                    if following:
                        store_values(l + 1, 0)
                        for r in range(4):
                            store_qk(l + 1, 0, r)

                e.preload_act_table_set(LN_EXP)
                for i in range(2):
                    squares(0, 0, i)
                    inverse_norms(0, 0, i)
                store_values(0, 0)
                for r in range(4):
                    store_qk(0, 0, r)
                with e.Fori(0, DEPTH - 1) as l:
                    e.preload_act_table_set(LN_EXP)
                    attend(l)
                    forward(l, True)
                attend(DEPTH - 1)
                forward(DEPTH - 1, False)

            @block.vector
            def _(e):
                for signal in (s.xs, s.cosine, s.d_free, s.normed, s.total):
                    e.sem_inc(signal, START)

                def sum_squares(l, T, i):
                    n = (l * NT + T) * 2 + i
                    e.wait_ge(s.square, n + 1)
                    e.tensor_reduce(norm[:, 0, :], square[:, :, :], AX.X, ALU.add).then_inc(s.total, 1)

                def normalise(l, T, i):
                    n = (l * NT + T) * 2 + i
                    e.wait_ge(s.root, 2 * n + 2)
                    e.tensor_scalar(norm[:, 3, :], norm[:, 2, :], 1.0 / NORM_MIN, None, ALU.min).then_inc(s.bound, 1)
                    e.wait_ge(s.bound, n + 1)
                    e.tensor_tensor(qn[:, i, :, :], flat2(ps[:, 0:2, :]).rearrange("p (h d) -> p h d", h=LH),
                                    norm[:, 3, :].unsqueeze(2).to_broadcast([P, LH, LD]), ALU.mult).then_inc(s.qn, 1)
                    e.wait_ge(s.qn, n + 1)
                    if T == 0 and i == 0:
                        e.wait_ge(s.tab, START + (l + 1) * 4)
                    e.tensor_tensor(cosine[:, i, :, :], qn[:, i, :, :],
                                    tab[:, 2 * i, T, :].unsqueeze(1).to_broadcast([P, LH, LD]), ALU.mult).then_inc(s.cosine, 1)

                def halve(l, T, r):
                    e.wait_ge(s.t_free, START + l * (6 * NT) + turn_index(T, r) + 1)
                    j = slice(4 * (r % 2), 4 * (r % 2) + 4)
                    if r < 2:
                        blocks = qTb[:, T % 2, j, :].rearrange("p j (w two q) -> p j w two q", two=2, q=WIN)
                        for i, half in ((0, slice(0, LD)), (1, slice(LD, P))):
                            ins = e.tensor_copy(blocks[half, :, :, i, :],
                                                qT[half, T % 2, j, i, :].rearrange("p j (w q) -> p j w q", q=WIN))
                    else:
                        ins = e.tensor_copy(kTb[:, T % 2, j, :], kT[:, T % 2, j, :])
                    ins.then_inc(s.half, 1)

                def maxima(l, T, r):
                    n = l * (4 * NT) + d_index(T, r)
                    e.wait_ge(s.d_ready, START + n + 1)
                    e.tensor_reduce(nmax[:, 8 * r:8 * r + 8], ps[:, 4 - r, :].rearrange("p (h k) -> p h k", h=8), AX.X, ALU.max,
                                    negate=True).then_inc(s.d_free, 1)

                def max_rows(l, T):
                    n = l * (4 * NT) + d_index(T, 2)
                    m = l * NT + T
                    e.wait_ge(s.d_ready, START + n + 1)
                    e.wait_ge(mrow_stored[T % 2], START + (l * (NT // 2) + T // 2) * 32)
                    e.tensor_copy(msplit[:, T % 2, 0, :], ps[0:LH, 4, 0:P]).then_inc(s.split, 1)
                    e.wait_ge(s.split, m + 1)
                    e.tensor_tensor(msplit[:, T % 2, 1, :], ps[0:LH, 4, 0:P], msplit[:, T % 2, 0, :], ALU.subtract)\
                        .then_inc(s.d_free, 1)

                def residual(l, T):
                    n = l * (4 * NT) + d_index(T, 3)
                    e.wait_ge(s.d_ready, START + n + 1)
                    e.tensor_tensor(X[:, T * P:(T + 1) * P], X[:, T * P:(T + 1) * P], ps[:, 4, 0:P], ALU.add)\
                        .then_inc(s.d_free, 1)

                def outputs(l, T, g):
                    n = (l * NT + T) * LG + g
                    e.wait_ge(s.pv_done, START + n + 2)
                    m = ps[:, 7, 0:QG * VL].rearrange("p (h w) -> p h w", h=QG)
                    e.reciprocal(rcp[:, :], m[:, :, LD]).then_inc(s.rcp, 1)
                    e.wait_ge(s.rcp, n + 1)
                    e.tensor_tensor(o_tok[:, T % 2, QG * g:QG * (g + 1), :], m[:, :, 0:LD],
                                    rcp[:, :].unsqueeze(2).to_broadcast([P, QG, LD]), ALU.mult).then_inc(s.normed, 1)
                    e.wait_ge(s.normed, START + n + 1)

                def attend(l):
                    for T in range(NT):
                        ahead = T + 1 < NT
                        maxima(l, T, 0)
                        maxima(l, T, 1)
                        max_rows(l, T)
                        if ahead:
                            sum_squares(l, T + 1, 0)
                            normalise(l, T + 1, 0)
                        if T:
                            residual(l, T - 1)
                        if ahead:
                            sum_squares(l, T + 1, 1)
                        outputs(l, T, 0)
                        if ahead:
                            normalise(l, T + 1, 1)
                            halve(l, T + 1, 0)
                        outputs(l, T, 1)
                        if ahead:
                            halve(l, T + 1, 1)
                        outputs(l, T, 2)
                        if ahead:
                            halve(l, T + 1, 2)
                            halve(l, T + 1, 3)
                        outputs(l, T, 3)
                    residual(l, NT - 1)
                    e.wait_ge(s.d_free, START + (l + 1) * (4 * NT))

                def hide(l, c, k):
                    n = l * NC + c
                    e.wait_ge(s.gelu, n * MT + k + 1)
                    e.wait_ge(s.up, n * MT + k + 1)
                    e.scalar_tensor_tensor(out=hidden[0:rows(k), k, :], in0=ps[0:rows(k), 4 + 2 * ((c * MT + k) % 2), :],
                                           scalar=b_1[0:rows(k), 0, k:k + 1], in1=gelu[0:rows(k), k, :],
                                           op0=ALU.add, op1=ALU.mult).then_inc(s.hidden, 1)

                def add_output(l, c):
                    n = l * NC + c
                    lo, hi = c * CH, (c + 1) * CH
                    e.wait_ge(s.y, n + 1)
                    e.scalar_tensor_tensor(out=X[:, lo:hi], in0=ps[:, 7, :], scalar=vec[:, 2:3], in1=X[:, lo:hi],
                                           op0=ALU.add, op1=ALU.add).then_inc(s.summed, 1)
                    e.wait_ge(s.summed, n + 1)
                    e.tensor_copy(XS[0:P // 2, lo:hi], X[0:P // 2, lo:hi]).then_inc(s.xs, 1)
                    lo = max(lo, 1)
                    e.tensor_copy(XS[P // 2:P, lo:hi], X[P // 2:P, lo - 1:hi - 1]).then_inc(s.xs, 1)

                def forward(l, following):
                    shift_tokens(e, XS, X, s.xs)
                    e.wait_ge(s.xs, START + l * SHIFTS + 2)
                    for c in range(NC):
                        cols = slice(c * CH, (c + 1) * CH)
                        e.wait_ge(s.mean, l * NC + c + 1)
                        e.tensor_tensor(xn[:, cols], XS[:, cols], ps[:, 3 + c, :], ALU.subtract).then_inc(s.centred, 1)
                    e.wait_ge(s.w_mlp, (l + 1) * 192)
                    for c in range(NC):
                        n = l * NC + c
                        cols = slice(c * CH, (c + 1) * CH)
                        e.wait_ge(s.rstd, n + 1)
                        e.scalar_tensor_tensor(out=xn[:, cols], in0=xn[:, cols], scalar=vec[:, 0:1], in1=ln_rstd[:, cols],
                                               op0=ALU.mult, op1=ALU.mult).then_inc(s.xn, 1)
                        e.wait_ge(s.xn, 2 * n + 1)
                        e.tensor_scalar(xn[:, cols], xn[:, cols], vec[:, 1:2], None, ALU.add).then_inc(s.xn, 1)
                    for c in range(NC):
                        if c:
                            add_output(l, c - 1)
                        for k in range(MT):
                            hide(l, c, k)
                        if following and c >= NC - 2:
                            sum_squares(l + 1, 0, c - (NC - 2))
                            normalise(l + 1, 0, c - (NC - 2))
                    add_output(l, NC - 1)
                    e.wait_ge(s.xs, START + (l + 1) * SHIFTS)
                    if following:
                        for r in range(4):
                            halve(l + 1, 0, r)

                for i in range(2):
                    sum_squares(0, 0, i)
                    normalise(0, 0, i)
                for r in range(4):
                    halve(0, 0, r)
                with e.Fori(0, DEPTH - 1) as l:
                    attend(l)
                    forward(l, True)
                attend(DEPTH - 1)
                forward(DEPTH - 1, False)


def tables():
    import numpy as np
    bf16 = mybir.dt.np(mybir.dt.bfloat16)
    ident = np.eye(P, dtype=np.float32)
    i = np.arange(P)
    inv = (1.0 / 10000.0 ** (np.arange(0, HD, 2, dtype=np.float32) / np.float32(HD))).astype(np.float32)
    freq = (np.arange(N, dtype=np.float32)[:, None] * inv[None, :]).astype(np.float32)
    rope = lambda f: np.ascontiguousarray(np.tile(np.repeat(f(freq), 2, axis=1), (1, H)).T.astype(np.float32))
    mask = np.where(i[None, :] > i[:, None], -1e30, 0.0)
    half = np.arange(0, LD, 2, dtype=np.float32)
    token = np.arange(N, dtype=np.float32)
    lfreq = token[:, None] * (1.0 / 10000.0 ** (half / np.float32(LD))).astype(np.float32)[None, :]
    lfreq = np.concatenate([lfreq, lfreq], -1).astype(np.float32)
    growth = ((half + 0.4 * LD) / (1.4 * LD)).astype(np.float64)
    growth = np.concatenate([growth, growth])
    power = (token % CH - CH // 2).astype(np.float64) / (WIN // 2)
    scale = growth[None, :] ** power[:, None]
    sign = np.where(np.arange(LD) < ROT, -1.0, 1.0)
    cos, sin = np.cos(lfreq), np.sin(lfreq) * sign
    base = np.stack([cos * scale * QK_SCALE, sin * scale * QK_SCALE, cos / scale, sin / scale]).astype(np.float32)
    base = np.ascontiguousarray(base.reshape(4, NT, P, LD).transpose(2, 0, 1, 3))
    key = np.arange(2 * WIN)[None, :]
    query = (i % WIN)[:, None]
    seen = (query <= key) & (key <= query + WIN)
    seen0 = seen & ((i[:, None] >= 2 * WIN) | (key >= WIN))
    low = lambda m: np.where(m, 0.0, -1e30)
    mask_c = np.stack([np.tile(low(seen), (1, 8)), np.tile(np.concatenate([low(seen0), low(seen)], 1), (1, 4))], 1)
    ahead = i[None, :] - i[:, None]
    mask_d = np.tile(low((ahead >= 0) & (ahead <= WIN)), (1, QG))
    mask_p = np.zeros((P, LH * WIN))
    mask_p[P - WIN:] = np.tile(low(np.arange(WIN)[None, :] <= np.arange(WIN)[:, None]), (1, LH))
    const = np.zeros((P, 4), np.float32)
    const[:, 0], const[:, 1], const[:, 2] = LN_TINY, 0.5 * np.log(LN_RANGE), EPS
    const[:, 3] = growth[i % LD] ** (CH // (WIN // 2))
    return {
        "c_base": base, "c_mask_c": mask_c.astype(bf16), "c_mask_d": mask_d.astype(bf16),
        "c_mask_p": mask_p.astype(bf16), "c_const": const,
        "c_ident": ident, "c_identb": ident.astype(bf16),
        "c_mask_qk": mask.astype(bf16), "c_mask_kq": np.ascontiguousarray(mask.T).astype(bf16),
        "c_cos": rope(np.cos), "c_sin": rope(np.sin),
    }


def program(nc, a, out):
    with ExitStack() as outer:
        t, d = Names(), Names()
        sbo = lambda name, shape, dt=F32: outer.enter_context(nc.sbuf_tensor(name, shape, dt))
        t.x = sbo("x", [P, NT, P])
        t.X = sbo("X", [P, N])
        t.ident = sbo("ident", [P, P])
        t.stat = sbo("stat", [P, 48])
        t.identb = sbo("identb", [P, P], BF16)
        t.ps = outer.enter_context(nc.psum_tensor("ps", [P, 8, CH], F32))
        d.rope_cos, d.rope_sin = a["c_cos"], a["c_sin"]
        d.pieces = nc.dram_tensor("pieces", [2, 3, P, N], BF16).ap()
        rows = lambda x: x.rearrange("a (t p) n -> (a p) t n", p=P)
        with ExitStack() as ctx:
            sb = lambda name, shape, dt=F32: ctx.enter_context(nc.sbuf_tensor(name, shape, dt))
            t.V = sb("V", [P, NT, H * VW + 32 - VW])
            t.mask_qk = sb("mask_qk", [P, P], BF16)
            t.mask_kq = sb("mask_kq", [P, P], BF16)
            t.wo = sb("wo", [P, P])
            loaded = ctx.enter_context(nc.semaphore("loaded"))
            with nc.Block() as block:
                @block.sync
                def _(e):
                    e.dma_start(t.x[:, :, :], rows(a["L0_attn_x"])).then_inc(loaded, 16)
                    e.dma_start(t.ident[:, :], a["c_ident"]).then_inc(loaded, 16)
                    e.dma_start(t.identb[:, :], a["c_identb"]).then_inc(loaded, 16)
                    e.dma_start(t.mask_qk[:, :], a["c_mask_qk"]).then_inc(loaded, 16)
                    e.dma_start(t.mask_kq[:, :], a["c_mask_kq"]).then_inc(loaded, 16)
                    e.wait_ge(loaded, 80)
            w = a["L0_attn_w_qkv"]
            attention_inputs(nc, t, "a0_", d, [w[:, i * P:(i + 1) * P] for i in range(3)], a["L0_attn_w_proj"], False)
            attention(nc, t, "a0_", d, False)
            fp4_feed_forward(nc, t, a)
            attention_inputs(nc, t, "a1_", d, [a["L1_attn_Wq"], a["L1_attn_Wk"], a["L1_attn_Wv"]], a["L1_attn_Wo"], True)
            attention(nc, t, "a1_", d, True)
        layers(nc, t, a)
        with ExitStack() as ctx:
            s = semaphores(ctx, nc, "end_", "transposed copied stored")
            with nc.Block() as block:
                @block.tensor
                def _(e):
                    for i in range(NT):
                        e.transpose(t.ps[:, i // TC, (i % TC) * P:(i % TC + 1) * P], t.X[:, i * P:(i + 1) * P],
                                    t.ident[:, :]).then_inc(s.transposed, 1)

                @block.vector
                def _(e):
                    for c in range(NC):
                        e.wait_ge(s.transposed, TC * (c + 1))
                        e.tensor_tensor(t.x[:, TC * c:TC * (c + 1), :], t.x[:, TC * c:TC * (c + 1), :],
                                        t.ps[:, c, :].rearrange("p (q n) -> p q n", q=TC), ALU.add)\
                            .then_inc(s.copied, 1)

                @block.sync
                def _(e):
                    for c in range(NC):
                        e.wait_ge(s.copied, c + 1)
                        e.dma_start(rows(out)[:, TC * c:TC * (c + 1), :], t.x[:, TC * c:TC * (c + 1), :]).then_inc(s.stored, 16)
                    e.wait_ge(s.stored, 16 * NC)


_INS = ["L0_attn_x", "L0_attn_w_qkv", "L0_attn_w_proj", "L0_ffn_w_gate", "L0_ffn_w_up", "L0_ffn_w_down", "L1_attn_Wq",
        "L1_attn_Wk", "L1_attn_Wv", "L1_attn_Wo", "L1_ffn_Wqkv", "L1_ffn_q_scale", "L1_ffn_k_scale", "L1_ffn_Wo",
        "L1_ffn_ln_g", "L1_ffn_ln_b", "L1_ffn_W1", "L1_ffn_b1", "L1_ffn_W2", "L1_ffn_b2"]


def kernel(**inputs):
    import numpy as np
    import concourse.bacc as bacc
    from concourse.bass_utils import run_bass_kernel_spmd

    nc = bacc.Bacc("TRN2", target_bir_lowering=False, num_devices=1)
    arrays = {name: np.ascontiguousarray(inputs[name]) for name in _INS}
    arrays.update(tables())
    named = {f"in_{name}_dram": value for name, value in arrays.items()}
    a = {name: nc.dram_tensor(f"in_{name}_dram", value.shape, mybir.dt.from_np(value.dtype), kind="ExternalInput").ap()
         for name, value in arrays.items()}
    out = nc.dram_tensor("out_0_dram", (1, N, P), F32, kind="ExternalOutput").ap()
    program(nc, a, out)
    r = run_bass_kernel_spmd(nc, [named], core_ids=[0])
    return r.results[0]["out_0_dram"]
```

```python
from collections import namedtuple
from contextlib import ExitStack

import concourse.bass as bass
from concourse import mybir

F32 = mybir.dt.float32
BF16 = mybir.dt.bfloat16
ALU = mybir.AluOpType
ACT = mybir.ActivationFunctionType
AX = mybir.AxisListType

P = 128
N = 2048
NT = N // P
CH = 512
NC = N // CH
TC = CH // P
H = 16
EPS = 1e-5

HD = P // H
G = 4
NG = H // G
VW = HD + 1
TERMS = [(0, 0), (0, 1), (0, 2), (1, 0), (1, 1), (2, 0)]
MROW = HD * len(TERMS)
KB = 4
LEAD = 3
ONES = 1.0019378662109375


def layer_norm(nc, t, x, xn, sq, s, n):
    def vector(e):
        e.tensor_reduce(t.stat[:, 0:n], x, AX.X, ALU.add).then_inc(s.ln_v, 1)
        e.wait_ge(s.ln_v, 1)
        e.tensor_scalar(t.stat[:, 16:16 + n], t.stat[:, 0:n], -1.0 / P, None, ALU.mult).then_inc(s.ln_v, 1)
        e.wait_ge(s.ln_v, 2)
        e.tensor_tensor(xn, x, t.stat[:, 16:16 + n].unsqueeze(2).to_broadcast([P, n, P]), ALU.add).then_inc(s.ln_v, 1)
        e.wait_ge(s.ln_a, 1)
        e.tensor_reduce(t.stat[:, 0:n], sq, AX.X, ALU.add).then_inc(s.ln_v, 1)
        e.wait_ge(s.ln_v, 4)
        e.tensor_scalar(t.stat[:, 16:16 + n], t.stat[:, 0:n], 1.0 / P, EPS, ALU.mult, ALU.add).then_inc(s.ln_v, 1)
        e.wait_ge(s.ln_a, 2)
        e.reciprocal(t.stat[:, 0:n], t.stat[:, 32:32 + n]).then_inc(s.ln_v, 1)
        e.wait_ge(s.ln_v, 6)
        e.tensor_tensor(xn, xn, t.stat[:, 0:n].unsqueeze(2).to_broadcast([P, n, P]), ALU.mult).then_inc(s.ln_v, 1)

    def scalar(e):
        e.wait_ge(s.ln_v, 3)
        e.activation(sq, xn, ACT.Square).then_inc(s.ln_a, 1)
        e.wait_ge(s.ln_v, 5)
        e.activation(t.stat[:, 32:32 + n], t.stat[:, 16:16 + n], ACT.Sqrt).then_inc(s.ln_a, 1)

    return vector, scalar


class Names:
    pass


def semaphores(ctx, nc, prefix, names):
    return namedtuple("Semaphores", names)(*[ctx.enter_context(nc.semaphore(prefix + name)) for name in names.split()])


PIECES = [(0, 0), (0, 1), (1, 0), (0, 2), (1, 1), (1, 2)]
RESTS = [(0, 0), (0, 1), (1, 0), (1, 1)]


def attention_inputs(nc, t, prefix, d, wq_dram, wo_dram, out_by_in):
    with ExitStack() as ctx:
        s = semaphores(ctx, nc, prefix, "ln_v ln_a load xT xT_a xT_b wT wprep proj rot turned rest piece v v_set store")
        xn = ctx.enter_context(nc.sbuf_tensor(prefix + "xn", [P, NT, P], F32))
        sq = ctx.enter_context(nc.sbuf_tensor(prefix + "sq", [P, NT, P], F32))
        xT = ctx.enter_context(nc.sbuf_tensor(prefix + "xT", [P, N], F32))
        cos = ctx.enter_context(nc.sbuf_tensor(prefix + "cos", [P, N], F32))
        sin = ctx.enter_context(nc.sbuf_tensor(prefix + "sin", [P, N], F32))
        rot = ctx.enter_context(nc.sbuf_tensor(prefix + "rot", [P, 2, 2, N], F32))
        piece = ctx.enter_context(nc.sbuf_tensor(prefix + "piece", [P, 6, N], BF16))
        wraw = ctx.enter_context(nc.sbuf_tensor(prefix + "wraw", [P, 4, P], F32))
        wall = ctx.enter_context(nc.sbuf_tensor(prefix + "wall", [P, 3, P], F32))
        wrot = ctx.enter_context(nc.sbuf_tensor(prefix + "wrot", [P, 2, P], F32))
        ps = t.ps
        ln_vector, ln_scalar = layer_norm(nc, t, t.x[:, :, :], xn[:, :, :], sq[:, :, :], s, NT)

        with nc.Block() as block:
            @block.sync
            def _(e):
                for i, w in enumerate(wq_dram):
                    e.dma_start(wraw[:, i, :], w).then_inc(s.load, 16)
                e.dma_start(wraw[:, 3, :], wo_dram).then_inc(s.load, 16)
                e.dma_start(cos[:, :], d.rope_cos).then_inc(s.load, 16)
                e.dma_start(sin[:, :], d.rope_sin).then_inc(s.load, 16)
                for n, (i, j) in enumerate(PIECES):
                    e.wait_ge(s.piece, n + 1)
                    e.dma_start(d.pieces[i, j], piece[:, 3 * i + j, :]).then_inc(s.store, 16)
                e.wait_ge(s.store, 96)

            @block.tensor
            def _(e):
                if out_by_in:
                    e.wait_ge(s.load, 96)
                    for i in range(4):
                        e.transpose(ps[:, 4, i * P:(i + 1) * P], wraw[:, i, :], t.ident[:, :]).then_inc(s.wT, 1)
                e.wait_ge(s.ln_v, 7)
                for i in range(NT):
                    e.transpose(ps[:, i // TC, (i % TC) * P:(i % TC + 1) * P], xn[:, i, :], t.ident[:, :]).then_inc(s.xT, 1)
                e.wait_ge(s.xT_a, 1)
                e.wait_ge(s.xT_b, 1)
                e.wait_ge(s.wprep, 5)
                for i in range(2):
                    if i:
                        e.wait_ge(s.rot, 1)
                    for c in range(NC):
                        e.matmul(ps[:, c, :], wall[:, i, :], xT[:, c * CH:(c + 1) * CH], start=True, stop=True)\
                            .then_inc(s.proj, 1)
                    if i:
                        e.wait_ge(s.rot, 2)
                    for c in range(NC):
                        e.matmul(ps[:, 4 + c, :], wrot[:, i, :], xT[:, c * CH:(c + 1) * CH], start=True, stop=True)\
                            .then_inc(s.proj, 1)
                e.wait_ge(s.rot, 3)
                for i in range(NT):
                    e.matmul(ps[:, i // TC, (i % TC) * P:(i % TC + 1) * P], xT[:, i * P:(i + 1) * P], wall[:, 2, :],
                             start=True, stop=True).then_inc(s.v, 1)

            @block.vector
            def _(e):
                ln_vector(e)
                if out_by_in:
                    e.wait_ge(s.wT, 4)
                    w = ps[:, 4, :].rearrange("p (i n) -> p i n", i=4)
                else:
                    e.wait_ge(s.load, 96)
                    w = wraw
                e.tensor_scalar(wall[:, 0, :], w[:, 0, :], HD ** -0.5, None, ALU.mult).then_inc(s.wprep, 1)
                e.tensor_copy(wall[:, 1:3, :], w[:, 1:3, :]).then_inc(s.wprep, 1)
                e.tensor_copy(t.wo[:, :], w[:, 3, :]).then_inc(s.wprep, 1)
                e.wait_ge(s.wprep, 3)
                pair = lambda a: a.rearrange("p i (n two) -> p i n two", two=2)
                e.tensor_scalar(pair(wrot[:, :, :])[:, :, :, 0], pair(wall[:, 0:2, :])[:, :, :, 1], -1.0, None,
                                ALU.mult).then_inc(s.wprep, 1)
                e.tensor_copy(pair(wrot[:, :, :])[:, :, :, 1], pair(wall[:, 0:2, :])[:, :, :, 0]).then_inc(s.wprep, 1)
                e.wait_ge(s.xT, 8)
                e.tensor_copy(xT[:, 0:N // 2], ps[:, 0:2, :].rearrange("p b n -> p (b n)")).then_inc(s.xT_a, 1)

                def products(i):
                    for b, table in ((0, cos), (1, sin)):
                        e.wait_ge(s.proj, 8 * i + 4 * b + 4)
                        e.tensor_tensor(rot[:, i, b, :], ps[:, 4 * b:4 * b + 4, :].rearrange("p b n -> p (b n)"), table[:, :],
                                        ALU.mult).then_inc(s.rot, 1)

                def add(i):
                    e.wait_ge(s.rot, 2 * i + 2)
                    e.tensor_tensor(rot[:, i, 0, :], rot[:, i, 0, :], rot[:, i, 1, :], ALU.add).then_inc(s.turned, 1)

                def take_off(i, j):
                    e.wait_ge(s.piece, PIECES.index((i, j)) + 1)
                    e.tensor_tensor(rot[:, i, 0, :], rot[:, i, 0, :], piece[:, 3 * i + j, :], ALU.subtract).then_inc(s.rest, 1)

                products(0)
                add(0)
                products(1)
                take_off(0, 0)
                add(1)
                for i, j in RESTS[1:]:
                    take_off(i, j)

            @block.scalar
            def _(e):
                ln_scalar(e)
                e.wait_ge(s.xT, NT)
                e.copy(xT[:, N // 2:N], ps[:, 2:4, :].rearrange("p b n -> p (b n)")).then_inc(s.xT_b, 1)
                for i, j in PIECES:
                    if j:
                        e.wait_ge(s.rest, RESTS.index((i, j - 1)) + 1)
                    else:
                        e.wait_ge(s.turned, i + 1)
                    e.copy(piece[:, 3 * i + j, :], rot[:, i, 0, :]).then_inc(s.piece, 1)
                e.wait_ge(s.v, NT)
                e.wait_ge(s.v_set, 1)
                for b in range(NC):
                    e.copy(t.V[:, TC * b:TC * b + TC, 0:H * VW].rearrange("p t (h w) -> p t h w", w=VW)[:, :, :, 0:HD],
                           ps[:, b, :].rearrange("p (t h d) -> p t h d", t=TC, d=HD)).then_inc(s.xT_b, 1)

            @block.gpsimd
            def _(e):
                e.memset(t.V[:, :, :], 1.0).then_inc(s.v_set, 1)


def attention(nc, t, prefix, d, causal):
    units = [(c, g) for c in range(NC) for g in range(NG)]
    tiles_of = lambda c: TC * (c + 1) if causal else NT
    blocks_of = lambda c: c + 1 if causal else KB

    def max_blocks(u):
        c, g = units[u]
        out = []
        for qt in range(TC):
            for h in range(G):
                for b in range(blocks_of(c)):
                    last = causal and b == c
                    out.append((qt, h, b, P * (qt + 1) if last else CH, last))
        return out

    first_max = [0]
    first_step = [0]
    for u, (c, _) in enumerate(units):
        first_max.append(first_max[-1] + len(max_blocks(u)))
        first_step.append(first_step[-1] + tiles_of(c))

    plan = [[] for _ in range(first_step[-1])]
    start = []
    completes = {}
    for u in range(1, len(units)):
        blocks = list(enumerate(max_blocks(u)))
        at, until = first_step[u - 1] - LEAD, first_step[u] - LEAD
        for k, x in blocks:
            step = at + k * (until - at) // len(blocks)
            (plan[step] if step >= 0 else start).append((u, k, x))
        completes[until - 1] = u

    def quarter(step, i):
        blocks = plan[step]
        return blocks[len(blocks) * i // 4:len(blocks) * (i + 1) // 4]

    with ExitStack() as ctx:
        s = semaphores(ctx, nc, prefix, "fill clear stack_k0 stack_k1 stack_k2 stack_k3 stack_q0 stack_q1 stack_q2 stack_q3 scored reduced nmax split mrow_even mrow_odd st_ready exp_done pv_done os_done "
                       "misc_ready misc_used onorm rcp oT")
        stack_k = [s.stack_k0, s.stack_k1, s.stack_k2, s.stack_k3]
        stack_q = [s.stack_q0, s.stack_q1, s.stack_q2, s.stack_q3]
        mrow_stored = [s.mrow_even, s.mrow_odd]
        sb = lambda name, shape, dt=F32: ctx.enter_context(nc.sbuf_tensor(prefix + name, shape, dt))
        QS = sb("QS", [P, NC, H, CH], BF16)
        KS = sb("KS", [P, H, N], BF16)
        Pb = sb("Pb", [P, 2, G, CH])
        OS = sb("OS", [P, 2, CH])
        part = sb("part", [P, 2, G * TC, KB])
        nmax = sb("nmax", [P, 2, G * TC])
        mrow = sb("mrow", [G * TC, 2, 2, P], BF16)
        rcp = sb("rcp", [P, 2, TC * G])
        o_tok = sb("o_tok", [P, 2, TC, P])
        oT = sb("oT", [P, 2, CH])
        ps = t.ps
        O, MISC = ps[:, 6, :], ps[:, 7, :]

        with nc.Block() as block:
            @block.sync
            def _(e):
                def stack_keys(g):
                    heads = slice(G * g, G * (g + 1))
                    for j in range(len(TERMS)):
                        e.dma_start(KS[HD * j:HD * (j + 1), heads, :],
                                    d.pieces[1, TERMS[j][1]].rearrange("(h d) n -> d h n", d=HD)[:, heads, :])\
                            .then_inc(stack_k[g], 16)

                def stack_queries(c):
                    for j in range(len(TERMS)):
                        e.dma_start(QS[HD * j:HD * (j + 1), c, :, :],
                                    d.pieces[0, TERMS[j][0], :, c * CH:(c + 1) * CH].rearrange("(h d) n -> d h n", d=HD))\
                            .then_inc(stack_q[c], 16)

                e.wait_ge(s.fill, 1)
                stack_keys(0)
                e.wait_ge(s.clear, 1)
                stack_queries(0)
                for g in range(1, NG):
                    e.wait_ge(s.clear, 1 + g)
                    stack_keys(g)
                for c in range(1, NC):
                    e.wait_ge(s.clear, NG + c)
                    stack_queries(c)
                for u, (c, g) in enumerate(units):
                    e.wait_ge(s.split, 2 * u + 2)
                    for j in range(2):
                        e.dma_start(QS[MROW + j:MROW + j + 1, c, G * g:G * g + G, :].rearrange("p h n -> p (h n)"),
                                    mrow[:, u % 2, j, :]).then_inc(mrow_stored[u % 2], 16)

            @block.gpsimd
            def _(e):
                clear_queries = lambda c: e.memset(QS[:, c, :, :].rearrange("p h n -> p (h n)").bitcast(F32), 0.0)
                clear_queries(0).then_inc(s.clear, 1)
                for g in range(1, NG):
                    e.memset(KS[:, G * g:G * (g + 1), :].rearrange("p h n -> p (h n)").bitcast(F32), ONES).then_inc(s.clear, 1)
                for c in range(1, NC):
                    clear_queries(c).then_inc(s.clear, 1)

            @block.tensor
            def _(e):
                misc = 0

                def max_block(u, k, qt, h, b, width, masked):
                    c, g = units[u]
                    n = first_max[u] + k
                    if k == 0 and c == 0:
                        e.wait_ge(stack_k[g], 16 * len(TERMS))
                    if k == 0 and g == 0:
                        e.wait_ge(stack_q[c], 16 * len(TERMS))
                    if n >= 2:
                        e.wait_ge(s.reduced, n - 1)
                    bank = ps[:, 4 + n % 2, :]
                    head = G * g + h
                    if masked:
                        e.matmul(bank[:, width - P:width], t.identb[:, :], t.mask_qk[:, :], start=True, stop=False,
                                 skip_group_check=True)
                    mm = e.matmul(bank[:, 0:width], QS[:, c, head, qt * P:(qt + 1) * P],
                                  KS[:, head, b * CH:b * CH + width], start=not masked, stop=True,
                                  skip_group_check=masked)
                    mm.then_inc(s.scored, 1)

                def max_rows(u):
                    nonlocal misc
                    e.wait_ge(s.nmax, u + 1)
                    if misc:
                        e.wait_ge(s.misc_used, misc)
                    e.transpose(MISC[0:G * TC, 0:P], nmax[:, u % 2, :], t.ident[:, :]).then_inc(s.misc_ready, 1)
                    misc += 1

                def out_rows(u):
                    nonlocal misc
                    e.wait_ge(s.os_done, u + 1)
                    e.wait_ge(s.misc_used, misc)
                    for qt in range(TC):
                        tr = e.transpose(MISC[:, qt * P:(qt + 1) * P], OS[:, u % 2, qt * P:(qt + 1) * P], t.ident[:, :])
                    tr.then_inc(s.misc_ready, 1)
                    misc += 1

                def chunk_columns(c):
                    nonlocal misc
                    e.wait_ge(s.onorm, NG * (c + 1))
                    e.wait_ge(s.misc_used, misc)
                    for qt in range(TC):
                        tr = e.transpose(MISC[:, qt * P:(qt + 1) * P], o_tok[:, c % 2, qt, :], t.ident[:, :])
                    tr.then_inc(s.misc_ready, 1)
                    misc += 1

                def chunk_project(c):
                    nonlocal misc
                    e.wait_ge(s.misc_used, misc)
                    for qt in range(TC):
                        mm = e.matmul(MISC[:, qt * P:(qt + 1) * P], oT[:, c % 2, qt * P:(qt + 1) * P], t.wo[:, :],
                                      start=True, stop=True)
                    mm.then_inc(s.misc_ready, 1)
                    misc += 1

                def first_column(u, kt):
                    c = units[u][0]
                    return P * (kt - TC * c) if causal and kt >= TC * c else 0

                def values(u, kt):
                    c, g = units[u]
                    n = first_step[u] + kt
                    a = first_column(u, kt)
                    e.wait_ge(s.exp_done, 2 * n + 2)
                    if kt == 0 and u:
                        e.wait_ge(s.os_done, u)
                    for h in range(G):
                        w = VW * (G * g + h)
                        mm = e.matmul(O[32 * h:32 * h + 32, a:CH], t.V[:, kt, w:w + 32], Pb[:, n % 2, h, a:CH],
                                      start=(kt == 0), stop=(kt == tiles_of(c) - 1), skip_group_check=True)
                    mm.then_inc(s.pv_done, 1)

                for k, x in enumerate(max_blocks(0)):
                    max_block(0, k, *x)
                max_rows(0)
                for u, k, x in start:
                    max_block(u, k, *x)
                for u, (c, g) in enumerate(units):
                    e.wait_ge(mrow_stored[u % 2], 32 * (u // 2 + 1))
                    for kt in range(tiles_of(c)):
                        n = first_step[u] + kt
                        a = first_column(u, kt)
                        diagonal = causal and kt >= TC * c
                        for p in range(2):
                            if n:
                                e.wait_ge(s.exp_done, 2 * n - 1 + p)
                            for h in (2 * p, 2 * p + 1):
                                head = G * g + h
                                if diagonal:
                                    e.matmul(ps[:, h, a:a + P], t.identb[:, :], t.mask_kq[:, :], start=True,
                                             stop=False, skip_group_check=True)
                                mm = e.matmul(ps[:, h, a:CH], KS[:, head, kt * P:(kt + 1) * P],
                                              QS[:, c, head, a:CH], start=not diagonal, stop=True,
                                              skip_group_check=diagonal)
                            mm.then_inc(s.st_ready, 1)
                            for v, k, x in quarter(n, p):
                                max_block(v, k, *x)
                        if kt:
                            values(u, kt - 1)
                        for i in (2, 3):
                            for v, k, x in quarter(n, i):
                                max_block(v, k, *x)
                        if n - 1 in completes:
                            max_rows(completes[n - 1])
                        if u and kt == 1:
                            out_rows(u - 1)
                        if u and kt == 2 and g == 0:
                            chunk_columns(c - 1)
                        if u and kt == 3 and g == 0:
                            chunk_project(c - 1)
                    values(u, tiles_of(c) - 1)
                out_rows(len(units) - 1)
                chunk_columns(NC - 1)
                chunk_project(NC - 1)

            @block.scalar
            def _(e):
                for u, (c, g) in enumerate(units):
                    for kt in range(tiles_of(c)):
                        n = first_step[u] + kt
                        a = P * (kt - TC * c) if causal and kt >= TC * c else 0
                        for p in range(2):
                            e.wait_ge(s.st_ready, 2 * n + p + 1)
                            if n >= 2:
                                e.wait_ge(s.pv_done, n - 1)
                            e.activation(Pb[:, n % 2, 2 * p:2 * p + 2, a:CH], ps[:, 2 * p:2 * p + 2, a:CH], ACT.Exp)\
                                .then_inc(s.exp_done, 1)
                    e.wait_ge(s.pv_done, first_step[u + 1])
                    if u >= 2:
                        e.wait_ge(s.onorm, u - 1)
                    e.copy(OS[:, u % 2, :], O).then_inc(s.os_done, 1)

            @block.vector
            def _(e):
                e.memset(KS[:, 0:G, :].rearrange("p h n -> p (h n)").bitcast(F32), ONES).then_inc(s.fill, 1)
                misc = 0
                rcps = 0

                def reduce_block(u, k, qt, h, b, width, masked):
                    n = first_max[u] + k
                    e.wait_ge(s.scored, n + 1)
                    e.tensor_reduce(part[:, u % 2, h * TC + qt, b:b + 1], ps[:, 4 + n % 2, 0:width], AX.X, ALU.max)\
                        .then_inc(s.reduced, 1)

                def unit_maxima(u):
                    e.wait_ge(s.reduced, first_max[u + 1])
                    if u >= 2:
                        e.wait_ge(mrow_stored[u % 2], 32 * (u // 2))
                    e.tensor_reduce(nmax[:, u % 2, :], part[:, u % 2, :, 0:blocks_of(units[u][0])], AX.X, ALU.max,
                                    negate=True).then_inc(s.nmax, 1)

                def max_rows(u):
                    nonlocal misc
                    e.wait_ge(s.misc_ready, misc + 1)
                    if u >= 2:
                        e.wait_ge(mrow_stored[u % 2], 32 * (u // 2))
                    e.tensor_copy(mrow[:, u % 2, 0, :], MISC[0:G * TC, 0:P]).then_inc(s.split, 1)
                    e.wait_ge(s.split, 2 * u + 1)
                    e.tensor_tensor(mrow[:, u % 2, 1, :], MISC[0:G * TC, 0:P], mrow[:, u % 2, 0, :], ALU.subtract)\
                        .then_inc(s.split, 1)
                    e.wait_ge(s.split, 2 * u + 2)
                    e.engine_nop().then_inc(s.misc_used, 1)
                    misc += 1

                def out_rows(u):
                    nonlocal misc, rcps
                    c, g = units[u]
                    e.wait_ge(s.misc_ready, misc + 1)
                    m = MISC.rearrange("p (q h w) -> p q h w", q=TC, h=G)
                    e.reciprocal(rcp[:, u % 2, :].rearrange("p (q h) -> p q h", q=TC), m[:, :, :, HD]).then_inc(s.rcp, 1)
                    e.wait_ge(s.rcp, u + 1)
                    if g == 0 and c >= 2:
                        e.wait_ge(s.oT, 2 * (c - 1))
                    e.tensor_tensor(o_tok[:, c % 2, :, G * HD * g:G * HD * (g + 1)].rearrange("p q (h d) -> p q h d", h=G),
                                    m[:, :, :, 0:HD],
                                    rcp[:, u % 2, :].rearrange("p (q h) -> p q h", q=TC).unsqueeze(3)
                                    .to_broadcast([P, TC, G, HD]), ALU.mult).then_inc(s.onorm, 1)
                    e.wait_ge(s.onorm, u + 1)
                    e.engine_nop().then_inc(s.misc_used, 1)
                    misc += 1

                def chunk_columns(c):
                    nonlocal misc
                    e.wait_ge(s.misc_ready, misc + 1)
                    e.tensor_copy(oT[:, c % 2, :], MISC).then_inc(s.misc_used, 1)
                    misc += 1

                def chunk_project(c):
                    nonlocal misc
                    e.wait_ge(s.misc_ready, misc + 1)
                    e.tensor_tensor(t.x[:, TC * c:TC * (c + 1), :], t.x[:, TC * c:TC * (c + 1), :],
                                    MISC.rearrange("p (q n) -> p q n", q=TC), ALU.add).then_inc(s.oT, 2)
                    e.wait_ge(s.oT, 2 * (c + 1))
                    e.engine_nop().then_inc(s.misc_used, 1)
                    misc += 1

                for k, x in enumerate(max_blocks(0)):
                    reduce_block(0, k, *x)
                unit_maxima(0)
                max_rows(0)
                for u, k, x in start:
                    reduce_block(u, k, *x)
                for u, (c, g) in enumerate(units):
                    for kt in range(tiles_of(c)):
                        n = first_step[u] + kt
                        for v, k, x in plan[n]:
                            reduce_block(v, k, *x)
                        if n - 1 in completes:
                            max_rows(completes[n - 1])
                        if n in completes:
                            unit_maxima(completes[n])
                        if u and kt == 1:
                            out_rows(u - 1)
                        if u and kt == 2 and g == 0:
                            chunk_columns(c - 1)
                        if u and kt == 3 and g == 0:
                            chunk_project(c - 1)
                out_rows(len(units) - 1)
                chunk_columns(NC - 1)
                chunk_project(NC - 1)


FI = 352
KT = -(-FI // P)
KL = FI - (KT - 1) * P
QB = 16
SCALE_MIN = 1e-12


def quantizer(e, t, link, chain):
    def quantize(out, src, magnitude, sign, n):
        nb = n // QB
        blocks = lambda a: a.rearrange("p (b k) -> p b k", k=QB)
        wide = lambda a: a.unsqueeze(2).to_broadcast([P, nb, QB])
        top, scale, inverse = t.q_top[:, 0:nb], t.q_scale[:, 0:nb], t.q_inverse[:, 0:nb]
        ratio, halves = t.q_ratio[:, 0:n], t.q_halves[:, 0:n]
        link(e.tensor_reduce(top, blocks(src), AX.X, ALU.max, apply_absolute_value=True), chain)
        link(e.tensor_scalar(scale, top, 1.0 / 6.0, SCALE_MIN, ALU.mult, ALU.max), chain)
        link(e.reciprocal(inverse, scale), chain)
        link(e.tensor_tensor(blocks(ratio), blocks(magnitude), wide(inverse), ALU.mult), chain)
        link(e.tensor_scalar(halves, ratio, 5.0, 2.0, ALU.is_gt, ALU.mult), chain)
        for mid in (3.5, 2.5):
            link(e.scalar_tensor_tensor(out=halves, in0=ratio, scalar=mid, in1=halves, op0=ALU.is_gt, op1=ALU.add), chain)
        link(e.tensor_scalar(halves, halves, 2.0, None, ALU.mult), chain)
        for mid in (1.75, 1.25, 0.75, 0.25):
            link(e.scalar_tensor_tensor(out=halves, in0=ratio, scalar=mid, in1=halves, op0=ALU.is_gt, op1=ALU.add), chain)
        link(e.scalar_tensor_tensor(out=halves, in0=halves, scalar=0.5, in1=sign, op0=ALU.mult, op1=ALU.mult), chain)
        return e.tensor_tensor(blocks(out), blocks(halves), wide(scale), ALU.mult)
    return quantize


def linker(e):
    counts = {}

    def link(ins, sem):
        counts[sem] = counts.get(sem, 0) + 1
        ins.then_inc(sem, 1)
        e.wait_ge(sem, counts[sem])
    return link


def fp4_feed_forward(nc, t, a):
    WN = 2 * KT * P + FI
    GT = 4
    GN = GT * FI
    with ExitStack() as ctx:
        s = semaphores(ctx, nc, "f0_", "ln_v ln_a load clear chain wq xq w_abs x_abs wT wT_ev xT xT_ev gate_up silu "
                       "hidden h_abs hq hT hT_ev down added")
        sb = lambda name, shape, dt=F32: ctx.enter_context(nc.sbuf_tensor("f0_" + name, shape, dt))
        xn = sb("xn", [P, NT, P])
        xq = sb("xq", [P, NT, P])
        xT = sb("xT", [P, N])
        w = sb("w", [P, WN])
        wT = sb("wT", [P, 2, KT * P])
        dT = sb("dT", [P, KT, P])
        magnitude = sb("magnitude", [P, 2, N])
        sign = sb("sign", [P, 2, N])
        silu = sb("silu", [P, 2, FI])
        hidden = sb("hidden", [P, 3, GN])
        hT = sb("hT", [P, 2, KT * P])
        t.q_ratio, t.q_halves = sb("ratio", [P, N]), sb("halves", [P, N])
        t.q_top, t.q_scale, t.q_inverse = sb("top", [P, N // QB]), sb("scale", [P, N // QB]), sb("inverse", [P, N // QB])
        ps = t.ps
        flat = lambda ap: ap.rearrange("p b n -> p (b n)")
        rows = lambda k: P if k < KT - 1 else KL
        ln_vector, ln_scalar = layer_norm(nc, t, t.x[:, :, :], xn[:, :, :], xq[:, :, :], s, NT)

        with nc.Block() as block:
            @block.sync
            def _(e):
                e.wait_ge(s.clear, 1)
                for i, name in enumerate(("L0_ffn_w_gate", "L0_ffn_w_up")):
                    v = w[:, i * KT * P:(i + 1) * KT * P].rearrange("p (k n) -> p k n", n=P)
                    e.dma_start(v[:, 0:KT - 1, :], a[name][0:(KT - 1) * P, :].rearrange("(k p) n -> p k n", p=P))\
                        .then_inc(s.load, 16)
                    e.dma_start(v[0:KL, KT - 1, :], a[name][(KT - 1) * P:FI, :]).then_inc(s.load, 16)
                e.dma_start(w[:, 2 * KT * P:WN], a["L0_ffn_w_down"]).then_inc(s.load, 16)

            @block.gpsimd
            def _(e):
                e.memset(w[:, :], 0.0).then_inc(s.clear, 1)

            @block.tensor
            def _(e):
                e.wait_ge(s.wq, 1)
                for i in range(2):
                    for k in range(KT):
                        e.transpose(ps[:, i, k * P:(k + 1) * P], w[:, (i * KT + k) * P:(i * KT + k + 1) * P],
                                    t.ident[:, :]).then_inc(s.wT, 1)
                for k in range(KT):
                    at = 2 * KT * P + k * P
                    e.transpose(ps[0:rows(k), 2, k * P:(k + 1) * P], w[:, at:at + rows(k)], t.ident[:, :])\
                        .then_inc(s.wT, 1)
                e.wait_ge(s.xq, 1)
                for i in range(NT):
                    e.transpose(ps[:, 4 + i // TC, (i % TC) * P:(i % TC + 1) * P], xq[:, i, :], t.ident[:, :])\
                        .then_inc(s.xT, 1)
                e.wait_ge(s.wT_ev, 4)
                e.wait_ge(s.xT_ev, 1)

                def gate_up(i):
                    if i >= 2:
                        e.wait_ge(s.hidden, i - 1)
                    for j in range(2):
                        mm = e.matmul(ps[:, 2 * (i % 2) + j, 0:FI], xT[:, i * P:(i + 1) * P], wT[:, j, 0:FI],
                                      start=True, stop=True)
                    mm.then_inc(s.gate_up, 1)

                def down(i):
                    g = i // GT
                    e.wait_ge(s.hq, g + 1)
                    if i >= 2:
                        e.wait_ge(s.hT_ev, i - 1)
                    for k in range(KT):
                        at = (i % GT) * FI + k * P
                        tr = e.transpose(ps[0:rows(k), 4 + i % 2, k * P:(k + 1) * P], hidden[:, g % 3, at:at + rows(k)],
                                         t.ident[:, :])
                    tr.then_inc(s.hT, 1)

                def down_product(i):
                    g = i // GT
                    e.wait_ge(s.hT_ev, i + 1)
                    if g >= 2:
                        e.wait_ge(s.added, g - 1)
                    for k in range(KT):
                        mm = e.matmul(ps[:, 6 + g % 2, (i % GT) * P:(i % GT + 1) * P], hT[0:rows(k), i % 2, k * P:(k + 1) * P],
                                      dT[0:rows(k), k, :], start=(k == 0), stop=(k == KT - 1))
                    mm.then_inc(s.down, 1)

                for g in range(NT // GT + 2):
                    if g < NT // GT:
                        for i in range(GT * g, GT * g + GT):
                            gate_up(i)
                    if g >= 2:
                        for i in range(GT * (g - 2), GT * (g - 1)):
                            down(i)
                            if i > GT * (g - 2):
                                down_product(i - 1)
                        down_product(GT * (g - 1) - 1)

            @block.vector
            def _(e):
                link = linker(e)
                quantize = quantizer(e, t, link, s.chain)
                ln_vector(e)
                e.wait_ge(s.w_abs, 2)
                link(quantize(w[:, :], w[:, :], magnitude[:, 0, 0:WN], sign[:, 0, 0:WN], WN), s.wq)
                e.wait_ge(s.ln_v, 7)
                e.wait_ge(s.x_abs, 2)
                link(quantize(flat(xq[:, :, :]), flat(xn[:, :, :]), magnitude[:, 1, :], sign[:, 1, :], N), s.xq)
                e.wait_ge(s.xT, NT)
                e.tensor_copy(xT[:, :], flat(ps[:, 4:8, :])).then_inc(s.xT_ev, 1)

                def add_group(g):
                    e.wait_ge(s.down, GT * (g + 1))
                    e.tensor_tensor(t.x[:, GT * g:GT * (g + 1), :], t.x[:, GT * g:GT * (g + 1), :],
                                    ps[:, 6 + g % 2, :].rearrange("p (q n) -> p q n", q=GT), ALU.add).then_inc(s.added, 1)

                def multiply(g):
                    if g >= 3:
                        e.wait_ge(s.hT, GT * (g - 2))
                    for i in range(GT * g, GT * g + GT):
                        e.wait_ge(s.silu, i + 1)
                        e.tensor_tensor(hidden[:, g % 3, (i % GT) * FI:(i % GT + 1) * FI], silu[:, i % 2, :],
                                        ps[:, 2 * (i % 2) + 1, 0:FI], ALU.mult).then_inc(s.hidden, 1)

                multiply(0)
                for g in range(NT // GT):
                    if g + 1 < NT // GT:
                        multiply(g + 1)
                    e.wait_ge(s.hidden, GT * (g + 1))
                    e.wait_ge(s.h_abs, 2 * (g + 1))
                    link(quantize(hidden[:, g % 3, :], hidden[:, g % 3, :], magnitude[:, g % 2, 0:GN], sign[:, g % 2, 0:GN], GN),
                         s.hq)
                    if g:
                        add_group(g - 1)
                add_group(NT // GT - 1)
                e.wait_ge(s.added, NT // GT)

            @block.scalar
            def _(e):
                ln_scalar(e)
                e.wait_ge(s.load, 80)
                e.activation(magnitude[:, 0, 0:WN], w[:, :], ACT.Abs).then_inc(s.w_abs, 1)
                e.activation(sign[:, 0, 0:WN], w[:, :], ACT.Sign).then_inc(s.w_abs, 1)
                e.wait_ge(s.ln_v, 7)
                e.activation(magnitude[:, 1, :], flat(xn[:, :, :]), ACT.Abs).then_inc(s.x_abs, 1)
                e.activation(sign[:, 1, :], flat(xn[:, :, :]), ACT.Sign).then_inc(s.x_abs, 1)
                e.wait_ge(s.wT, 3 * KT)
                for i in range(2):
                    e.copy(wT[:, i, :], ps[:, i, 0:KT * P]).then_inc(s.wT_ev, 1)
                e.copy(dT[:, 0:KT - 1, :], ps[:, 2, 0:(KT - 1) * P].rearrange("p (k n) -> p k n", n=P)).then_inc(s.wT_ev, 1)
                e.copy(dT[0:KL, KT - 1, :], ps[0:KL, 2, (KT - 1) * P:KT * P]).then_inc(s.wT_ev, 1)

                def transposed(i):
                    e.wait_ge(s.hT, i + 1)
                    if i >= 2:
                        e.wait_ge(s.down, i - 1)
                    e.copy(hT[:, i % 2, 0:(KT - 1) * P], ps[:, 4 + i % 2, 0:(KT - 1) * P])
                    e.copy(hT[0:KL, i % 2, (KT - 1) * P:KT * P], ps[0:KL, 4 + i % 2, (KT - 1) * P:KT * P])\
                        .then_inc(s.hT_ev, 1)

                for g in range(NT // GT + 2):
                    if g < NT // GT:
                        for i in range(GT * g, GT * g + GT):
                            e.wait_ge(s.gate_up, i + 1)
                            if i >= 2:
                                e.wait_ge(s.hidden, i - 1)
                            e.activation(silu[:, i % 2, :], ps[:, 2 * (i % 2), 0:FI], ACT.Silu).then_inc(s.silu, 1)
                        e.wait_ge(s.hidden, GT * (g + 1))
                        if g >= 2:
                            e.wait_ge(s.hq, g - 1)
                        else:
                            e.wait_ge((s.wq, s.xq)[g], 1)
                        e.activation(magnitude[:, g % 2, 0:GN], hidden[:, g % 3, :], ACT.Abs).then_inc(s.h_abs, 1)
                        e.activation(sign[:, g % 2, 0:GN], hidden[:, g % 3, :], ACT.Sign).then_inc(s.h_abs, 1)
                    if g >= 2:
                        for i in range(GT * (g - 2), GT * (g - 1)):
                            transposed(i)


DEPTH = 6
WIN = 32
LD = 64
LH = 16
HALF = LH // 2
INNER = LH * LD
PAIRS = LH // 2
ROT = LD // 2
QG = 4
LG = LH // QG
VL = LD + 1
MI = 341
MT = -(-MI // P)
ML = MI - (MT - 1) * P
QK_SCALE = 8.0
LN_RANGE = 2.0 ** 24
LN_TINY = 2.0 ** -60
NORM_MIN = 1e-12
START = 1


TURNS = [(0, r) for r in range(4)]
DRAINS = []
for _T in range(NT):
    DRAINS += [(_T, 0), (_T, 1), (_T, 2)]
    if _T:
        TURNS += [(_T - 1, 4), (_T - 1, 5)]
        DRAINS += [(_T - 1, 3)]
    if _T + 1 < NT:
        TURNS += [(_T + 1, r) for r in range(4)]
TURNS += [(NT - 1, 4), (NT - 1, 5)]
DRAINS += [(NT - 1, 3)]


def turn_index(T, r):
    return TURNS.index((T, r))


def d_index(T, r):
    return DRAINS.index((T, r))


def shift_tokens(e, XS, X, signal):
    e.tensor_copy(XS[0:P // 2, :], X[0:P // 2, :]).then_inc(signal, 1)
    e.tensor_copy(XS[P // 2:P, 1:N], X[P // 2:P, 0:N - 1]).then_inc(signal, 1)


LN_EXP = "natural_log_exp_and_others"
VALUE_BANK = [7, 3, 4, 7]
MEAN_BANK = [0, 1, 0, 6]
VAR_BANK = [0, 1, 2, 7]
SHIFTS = 4 * NC


def layers(nc, t, a):
    with ExitStack() as ctx:
        s = semaphores(ctx, nc, "l_", "w_qkv w_tab w_o w_mlp xs tab a_ready square total root qn cosine v_done rotated "
                       "t_ready t_free d_ready d_free split mrow_even mrow_odd prev_ready prev_done st_ready exp_done pv_done normed "
                       "mean centred varied ln_sq rstd xn gate gelu up hidden y half log bound rcp summed")
        sb = lambda name, shape, dt=F32: ctx.enter_context(nc.sbuf_tensor("l_" + name, shape, dt))
        X, ps = t.X, t.ps
        XS = sb("XS", [P, N])
        w_qkv = sb("w_qkv", [P, 3 * INNER])
        w_o = sb("w_o", [P, PAIRS, P])
        w_1 = sb("w_1", [P, 2 * MI])
        w_2 = sb("w_2", [P, MT, P])
        b_1 = sb("b_1", [P, 2, MT])
        vec = sb("vec", [P, 3])
        scales = sb("scales", [P, 4, LD])
        base = sb("base", [P, 4, NT, LD])
        tab = sb("tab", [P, 4, NT, LD])
        square = sb("square", [P, LH, LD])
        norm = sb("norm", [P, 4, LH])
        qn = sb("qn", [P, 2, LH, LD])
        cosine = sb("cosine", [P, 2, LH, LD])
        sine = sb("sine", [P, LH, LD])
        hat = sb("hat", [P, 2, LH * LD])
        qT = sb("qT", [P, 2, PAIRS, 2, P])
        qTb = sb("qTb", [P, 2, PAIRS, 2 * P], BF16)
        kT = sb("kT", [P, 2, PAIRS, WIN + P])
        kTb = sb("kTb", [P, 2, PAIRS, WIN + P], BF16)
        V = sb("V", [P, 3, LH, VL])
        nmax = sb("nmax", [P, LH])
        msplit = sb("msplit", [LH, 2, 2, P], BF16)
        mrow = sb("mrow", [2, 2, LH * P], BF16)
        weights = sb("weights", [P, 2, QG * P])
        before = sb("before", [P, LH * WIN])
        rcp = sb("rcp", [P, QG])
        o_tok = sb("o_tok", [P, 2, LH, LD])
        oT = sb("oT", [P, PAIRS, P])
        xn = sb("xn", [P, N])
        gelu = sb("gelu", [P, MT, CH])
        mask_c = sb("mask_c", [P, 2, CH], BF16)
        mask_d = sb("mask_d", [P, CH], BF16)
        mask_p = sb("mask_p", [P, CH], BF16)
        ones2 = sb("ones2", [2, P], BF16)
        means = sb("means", [P, P])
        const = sb("const", [P, 4])
        mrow_stored = [s.mrow_even, s.mrow_odd]
        flat2 = lambda ap: ap.rearrange("p b n -> p (b n)")
        rows = lambda k: P if k < MT - 1 else ML
        tiles = lambda ap: ap.rearrange("p (i n) -> p i n", i=NT)
        hidden = o_tok[:, :, :, :].rearrange("p i h d -> p (i h d)")[:, 0:MT * CH].rearrange("p (k n) -> p k n", k=MT)
        ln_square = qn[:, :, :, :].rearrange("p i h d -> p (i h d)")
        ln_rstd = cosine[:, :, :, :].rearrange("p i h d -> p (i h d)")

        with ExitStack() as c0:
            s0 = semaphores(c0, nc, "l0_", "load xT x clear ln_v ln_a")
            ln_vector, ln_scalar = layer_norm(nc, t, t.x[:, :, :], tiles(xn[:, :]), tiles(ln_square), s0, NT)
            with nc.Block() as block:
                @block.sync
                def _(e):
                    for dst, name in ((base[:, :, :, :], "c_base"), (mask_c[:, :, :], "c_mask_c"), (mask_d[:, :], "c_mask_d"),
                                      (mask_p[:, :], "c_mask_p"), (const[:, :], "c_const")):
                        e.dma_start(dst, a[name]).then_inc(s0.load, 16)
                    e.wait_ge(s0.load, 80)

                @block.gpsimd
                def _(e):
                    e.memset(XS[:, :], 0.0).then_inc(s0.clear, 1)
                    e.memset(qT[:, :, :, :, :], 0.0)
                    e.memset(qTb[:, :, :, :], 0.0)
                    e.memset(kT[:, :, :, :], 0.0)
                    e.memset(kTb[:, :, :, :], 0.0)
                    e.memset(V[:, :, :, :], 1.0)
                    e.memset(ones2[:, :], 1.0)
                    e.memset(means[:, :], 1.0 / P)

                @block.tensor
                def _(e):
                    e.wait_ge(s0.ln_v, 7)
                    for i in range(NT):
                        e.transpose(ps[:, i // TC, (i % TC) * P:(i % TC + 1) * P], tiles(xn[:, :])[:, i, :], t.ident[:, :])\
                            .then_inc(s0.xT, 1)

                @block.scalar
                def _(e):
                    ln_scalar(e)

                @block.vector
                def _(e):
                    ln_vector(e)
                    e.wait_ge(s0.xT, NT)
                    e.tensor_copy(X[:, :], flat2(ps[:, 0:4, :])).then_inc(s0.x, 1)
                    e.wait_ge(s0.x, 1)
                    e.wait_ge(s0.clear, 1)
                    shift_tokens(e, XS, X, s0.x)

        with nc.Block() as block:
            @block.sync
            def _(e):
                e.sem_inc(s.mrow_even, START)
                e.sem_inc(s.mrow_odd, START)

                def load_weights(l):
                    e.wait_ge(s.a_ready, START + l * (6 * NT))
                    e.dma_start(w_qkv[:, :], a["L1_ffn_Wqkv"][l]).then_inc(s.w_qkv, 16)
                    e.wait_ge(s.tab, START + l * 4)
                    for i, name in enumerate(("L1_ffn_q_scale", "L1_ffn_k_scale")):
                        v = a[name][l].rearrange("(o d) -> o d", o=1)
                        e.dma_start(scales[:, 2 * i, :], v.partition_broadcast(P)).then_inc(s.w_tab, 16)
                        e.dma_start(scales[:, 2 * i + 1, 0:ROT], v[:, ROT:LD].partition_broadcast(P)).then_inc(s.w_tab, 16)
                        e.dma_start(scales[:, 2 * i + 1, ROT:LD], v[:, 0:ROT].partition_broadcast(P)).then_inc(s.w_tab, 16)
                    e.wait_ge(s.d_ready, START + l * (4 * NT))
                    e.dma_start(w_o[:, :, :], a["L1_ffn_Wo"][l].rearrange("(j p) n -> p j n", p=P)).then_inc(s.w_o, 16)

                def load_forward(l):
                    e.wait_ge(s.xs, START + l * SHIFTS)
                    e.dma_start(w_1[:, :], a["L1_ffn_W1"][l]).then_inc(s.w_mlp, 16)
                    w2 = a["L1_ffn_W2"][l]
                    full = (MT - 1) * P
                    e.dma_start(w_2[:, 0:MT - 1, :], w2[0:full, :].rearrange("(k p) n -> p k n", p=P)).then_inc(s.w_mlp, 16)
                    e.dma_start(w_2[0:ML, MT - 1, :], w2[full:MI, :]).then_inc(s.w_mlp, 16)
                    for i in range(2):
                        b1 = a["L1_ffn_b1"][l, i * MI:(i + 1) * MI]
                        for k in range(MT):
                            e.dma_start(b_1[0:rows(k), i, k:k + 1], b1[k * P:k * P + rows(k)].rearrange("(p o) -> p o", o=1))\
                                .then_inc(s.w_mlp, 16)
                    for i, name in enumerate(("L1_ffn_ln_g", "L1_ffn_ln_b", "L1_ffn_b2")):
                        e.dma_start(vec[:, i:i + 1], a[name][l].rearrange("(p o) -> p o", o=1)).then_inc(s.w_mlp, 16)

                def store_maxima(l):
                    for T in range(NT):
                        if T == 2:
                            load_forward(l)
                        e.wait_ge(s.d_free, START + l * (4 * NT) + d_index(T, 2) + 1)
                        for j in range(2):
                            e.dma_start(mrow[j:j + 1, T % 2, :], msplit[:, T % 2, j, :]).then_inc(mrow_stored[T % 2], 16)

                load_weights(0)
                if DEPTH > 1:
                    with e.Fori(0, DEPTH - 1) as l:
                        store_maxima(l)
                        load_weights(l + 1)
                store_maxima(DEPTH - 1)

            @block.gpsimd
            def _(e):
                e.sem_inc(s.tab, START)
                e.sem_inc(s.rotated, START)

                def rotate(l, T, i):
                    n = (l * NT + T) * 2 + i
                    e.wait_ge(s.qn, 2 * n + 2)
                    swap = qn[:, i, :, :]
                    table = tab[:, 2 * i + 1, T, :].unsqueeze(1).to_broadcast([P, LH, LD])
                    e.wait_ge(s.rotated, START + n * 3)
                    e.tensor_tensor(sine[:, :, 0:ROT], swap[:, :, ROT:LD], table[:, :, 0:ROT], ALU.mult).then_inc(s.rotated, 1)
                    e.tensor_tensor(sine[:, :, ROT:LD], swap[:, :, 0:ROT], table[:, :, ROT:LD], ALU.mult).then_inc(s.rotated, 1)
                    if i:
                        return
                    e.wait_ge(s.rotated, START + n * 3 + 2)
                    e.wait_ge(s.cosine, START + n + 1)
                    e.tensor_tensor(hat[:, i, :].rearrange("p (h d) -> p h d", h=LH), cosine[:, i, :, :], sine[:, :, :], ALU.add)\
                        .then_inc(s.rotated, 1)

                def begin(l):
                    e.wait_ge(s.w_tab, (l + 1) * 96)
                    e.wait_ge(s.cosine, START + l * (2 * NT))
                    e.wait_ge(s.rotated, START + l * (6 * NT))
                    for i in range(4):
                        e.tensor_tensor(tab[:, i, :, :], base[:, i, :, :],
                                        scales[:, i, :].unsqueeze(1).to_broadcast([P, NT, LD]), ALU.mult).then_inc(s.tab, 1)
                    e.wait_ge(s.tab, START + (l + 1) * 4)
                    for i in range(2):
                        rotate(l, 0, i)

                def tiles_after(l):
                    for T in range(1, NT):
                        for i in range(2):
                            rotate(l, T, i)

                begin(0)
                with e.Fori(0, DEPTH - 1) as l:
                    tiles_after(l)
                    begin(l + 1)
                tiles_after(DEPTH - 1)

            @block.tensor
            def _(e):
                e.sem_inc(s.pv_done, START + 1)
                e.sem_inc(s.a_ready, START)
                e.sem_inc(s.d_ready, START)

                def project(l, T, i, halves=(0, 1)):
                    n = l * NT + T
                    for b in halves:
                        if i:
                            e.wait_ge(s.qn, 2 * (2 * n + i) - 1 + b)
                        elif b == 0:
                            e.wait_ge(s.v_done, START + n)
                        at = i * INNER + b * CH
                        e.matmul(ps[:, b, :], XS[:, T * P:(T + 1) * P], w_qkv[:, at:at + CH], start=True, stop=True)\
                            .then_inc(s.a_ready, 1)

                def turn_qk(l, T, r):
                    i = r // 2
                    e.wait_ge(s.rotated, START + ((l * NT + T) * 2 + i) * 3 + 3)
                    turn_at(l, T, r, lambda j: hat[:, i, (4 * (r % 2) + j) * P:(4 * (r % 2) + j + 1) * P])

                def turn_at(l, T, r, source):
                    n = l * (6 * NT) + turn_index(T, r)
                    e.wait_ge(s.t_free, START + n)
                    for j in range(4):
                        tr = e.transpose(ps[:, 2, j * P:(j + 1) * P], source(j), t.ident[:, :])
                    tr.then_inc(s.t_ready, 1)

                def turn_o(l, T, r):
                    e.wait_ge(s.normed, START + (l * NT + T + 1) * LG)
                    flat = o_tok[:, T % 2, :, :].rearrange("p h d -> p (h d)")
                    turn_at(l, T, r, lambda j: flat[:, (4 * (r - 4) + j) * P:(4 * (r - 4) + j + 1) * P])

                def compact(l, T, r):
                    n = l * (4 * NT) + d_index(T, r)
                    if r == 0:
                        e.wait_ge(s.d_free, START + n)
                        if T:
                            e.wait_ge(s.normed, START + (l * NT + T - 1) * LG + 3)
                    e.wait_ge(s.half, (l * NT + T) * 4 + r + 3)
                    e.matmul(ps[:, 3 + r, :], t.identb[:, :], mask_c[:, 0 if T else 1, :], start=True, stop=False,
                             skip_group_check=True)
                    for k in range(4):
                        for w in range(4):
                            half = LD * (w % 2)
                            at = LD * (2 * k + w // 2)
                            mm = e.matmul(ps[half:half + LD, 3 + r, at:at + LD], qTb[:, T % 2, 4 * r + k, LD * w:LD * (w + 1)],
                                          kTb[:, T % 2, 4 * r + k, WIN * w:WIN * (w + 2)],
                                          start=False, stop=True, skip_group_check=True)
                    mm.then_inc(s.d_ready, 1)

                def max_rows(l, T):
                    e.wait_ge(s.d_free, START + l * (4 * NT) + d_index(T, 2))
                    e.transpose(ps[0:LH, 4, 0:P], nmax[:, :], t.ident[:, :]).then_inc(s.d_ready, 1)

                def out_project(l, T):
                    e.wait_ge(s.t_free, START + l * (6 * NT) + turn_index(T, 5) + 1)
                    if T == 0:
                        e.wait_ge(s.w_o, (l + 1) * 16)
                    e.wait_ge(s.d_free, START + l * (4 * NT) + d_index(T, 3))
                    for j in range(PAIRS):
                        mm = e.matmul(ps[:, 4, 0:P], w_o[:, j, :], oT[:, j, :], start=(j == 0), stop=(j == PAIRS - 1))
                    mm.then_inc(s.d_ready, 1)

                def scores_before(l, T):
                    e.wait_ge(s.prev_done, START + l * (NT - 1) + T - 1)
                    out = ps[P - WIN:P, 3, :]
                    e.matmul(out, t.identb[:, P - WIN:P], mask_p[:, :], start=True, stop=False, skip_group_check=True)
                    for j in range(PAIRS):
                        e.matmul(out[:, 2 * WIN * j:2 * WIN * (j + 1)], kT[:, T % 2, j, 0:WIN], qT[:, T % 2, j, :, 0:WIN],
                                 start=False, stop=False, skip_group_check=True)

                def less_maxima_before(l, T):
                    e.matmul(ps[P - WIN:P, 3, :].rearrange("p (j q) -> p j q", j=PAIRS), ones2[:, 0:WIN],
                             mrow[:, T % 2, :].rearrange("p (j q) -> p j q", j=PAIRS)[:, :, 0:2 * WIN],
                             start=False, stop=True, skip_group_check=True).then_inc(s.prev_ready, 1)

                def scores(l, T, g):
                    n = (l * NT + T) * LG + g
                    e.wait_ge(s.exp_done, START + n)
                    bank = ps[:, 5 + g % 2, :]
                    e.matmul(bank, t.identb[:, :], mask_d[:, :], start=True, stop=False, skip_group_check=True)
                    for k in range(QG // 2):
                        j = g * (QG // 2) + k
                        e.matmul(bank[:, 2 * P * k:2 * P * (k + 1)], kT[:, T % 2, j, WIN:WIN + P], qT[:, T % 2, j, :, :],
                                 start=False, stop=False, skip_group_check=True)

                def less_maxima(l, T, g):
                    rows2 = mrow[:, T % 2, :].rearrange("p (j w two q) -> p j two w q", j=PAIRS, two=2, q=WIN)
                    for k in range(QG // 2):
                        mm = e.matmul(ps[:, 5 + g % 2, 2 * P * k:2 * P * (k + 1)].rearrange("p (two w q) -> p two w q", two=2, q=WIN),
                                      ones2[:, :], rows2[:, g * (QG // 2) + k, :, :, :], start=False, stop=True,
                                      skip_group_check=True)
                    mm.then_inc(s.st_ready, 1)

                def values(l, T, g):
                    n = (l * NT + T) * LG + g
                    e.wait_ge(s.exp_done, START + n + 2)
                    bank = VALUE_BANK[g]
                    if g == 0:
                        e.wait_ge(s.normed, START + n)
                        if T:
                            e.wait_ge(s.prev_done, START + l * (NT - 1) + T)
                    elif g == 2 and T:
                        e.wait_ge(s.d_free, START + l * (4 * NT) + d_index(T - 1, 3) + 1)
                    elif g == 3:
                        e.wait_ge(s.normed, START + n - 2)
                    for k in range(QG):
                        h = QG * g + k
                        mm = e.matmul(ps[:, bank, VL * k:VL * (k + 1)], weights[:, g % 2, P * k:P * (k + 1)], V[:, T % 3, h, :],
                                      start=True, stop=(T == 0), skip_group_check=True)
                        if T:
                            mm = e.matmul(ps[0:WIN, bank, VL * k:VL * (k + 1)], before[P - WIN:P, WIN * h:WIN * (h + 1)],
                                          V[P - WIN:P, (T - 1) % 3, h, :], start=False, stop=True, skip_group_check=True)
                    mm.then_inc(s.pv_done, 1)

                def mean(l, c):
                    e.wait_ge(s.xs, START + l * SHIFTS + 2 * c + 2)
                    if c == 2:
                        e.wait_ge(s.centred, l * NC + 1)
                    e.matmul(ps[:, MEAN_BANK[c], :], means[:, :], XS[:, c * CH:(c + 1) * CH], start=True, stop=True)\
                        .then_inc(s.mean, 1)

                def variance(l, c):
                    e.wait_ge(s.ln_sq, l * NC + c + 1)
                    e.matmul(ps[:, VAR_BANK[c], :], means[:, :], ln_square[:, c * CH:(c + 1) * CH], start=True, stop=True)\
                        .then_inc(s.varied, 1)

                def attend(l):
                    e.wait_ge(s.xs, START + l * SHIFTS)
                    for r in range(2):
                        compact(l, 0, r)
                    for T in range(NT):
                        ahead = T + 1 < NT
                        if T:
                            turn_o(l, T - 1, 4)
                        if ahead:
                            project(l, T + 1, 0, halves=(0,))
                        max_rows(l, T)
                        if ahead:
                            project(l, T + 1, 0, halves=(1,))
                        if T:
                            turn_o(l, T - 1, 5)
                            scores_before(l, T)
                        scores(l, T, 0)
                        if T:
                            out_project(l, T - 1)
                        e.wait_ge(mrow_stored[T % 2], START + (l * (NT // 2) + T // 2 + 1) * 32)
                        e.wait_ge(s.v_done, START + l * NT + T + 1)
                        less_maxima(l, T, 0)
                        if T:
                            less_maxima_before(l, T)
                        if ahead:
                            project(l, T + 1, 1)
                        else:
                            mean(l, 0)
                            mean(l, 1)
                        scores(l, T, 1)
                        less_maxima(l, T, 1)
                        values(l, T, 0)
                        if ahead:
                            turn_qk(l, T + 1, 0)
                        scores(l, T, 2)
                        less_maxima(l, T, 2)
                        values(l, T, 1)
                        if ahead:
                            turn_qk(l, T + 1, 1)
                            project(l, T + 1, 2)
                        else:
                            mean(l, 2)
                        scores(l, T, 3)
                        less_maxima(l, T, 3)
                        if ahead:
                            turn_qk(l, T + 1, 2)
                        values(l, T, 2)
                        if ahead:
                            turn_qk(l, T + 1, 3)
                        values(l, T, 3)
                        if ahead:
                            compact(l, T + 1, 0)
                            compact(l, T + 1, 1)
                    turn_o(l, NT - 1, 4)
                    turn_o(l, NT - 1, 5)
                    out_project(l, NT - 1)

                def gate_up(l, c, k):
                    n = l * NC + c
                    bank = 3 + 2 * ((c * MT + k) % 2)
                    if k == 0:
                        e.wait_ge(s.xn, 2 * n + 2)
                    if c * MT + k >= 2:
                        e.wait_ge(s.hidden, n * MT + k - 1)
                    else:
                        e.wait_ge(s.centred, (l + 1) * NC)
                    for to, at, signal in ((bank, MI, s.gate), (bank + 1, 0, s.up)):
                        e.matmul(ps[0:rows(k), to, :], w_1[:, at + k * P:at + k * P + rows(k)], xn[:, c * CH:(c + 1) * CH],
                                 start=True, stop=True).then_inc(signal, 1)

                def down(l, c):
                    n = l * NC + c
                    e.wait_ge(s.hidden, (n + 1) * MT)
                    if c:
                        e.wait_ge(s.summed, n)
                    else:
                        e.wait_ge(s.rstd, (l + 1) * NC)
                    for k in range(MT):
                        mm = e.matmul(ps[:, 7, :], w_2[0:rows(k), k, :], hidden[0:rows(k), k, :],
                                      start=(k == 0), stop=(k == MT - 1))
                    mm.then_inc(s.y, 1)

                def forward(l, following):
                    for c in range(NC - 1):
                        e.wait_ge(s.centred, l * NC + NC - 1)
                        variance(l, c)
                    mean(l, NC - 1)
                    variance(l, NC - 1)
                    e.wait_ge(s.w_mlp, (l + 1) * 192)
                    for c in range(NC):
                        gate_up(l, c, 0)
                        if c:
                            down(l, c - 1)
                        gate_up(l, c, 1)
                        if following and c == NC - 1:
                            project(l + 1, 0, 1)
                        gate_up(l, c, 2)
                        if following and c == NC - 2:
                            e.wait_ge(s.w_qkv, (l + 2) * 16)
                            e.wait_ge(s.xs, START + l * SHIFTS + 2 * NC + 2)
                            project(l + 1, 0, 0)
                    down(l, NC - 1)
                    if following:
                        project(l + 1, 0, 2)
                        for r in range(4):
                            turn_qk(l + 1, 0, r)

                e.wait_ge(s.w_qkv, 16)
                for i in range(3):
                    project(0, 0, i)
                for r in range(4):
                    turn_qk(0, 0, r)
                with e.Fori(0, DEPTH - 1) as l:
                    attend(l)
                    forward(l, True)
                attend(DEPTH - 1)
                forward(DEPTH - 1, False)

            @block.scalar
            def _(e):
                e.sem_inc(s.exp_done, START + 1)
                e.sem_inc(s.v_done, START)
                e.sem_inc(s.t_free, START)
                e.sem_inc(s.prev_done, START)

                def squares(l, T, i):
                    n = (l * NT + T) * 2 + i
                    for b in range(2):
                        e.wait_ge(s.a_ready, START + (l * NT + T) * 6 + 2 * i + b + 1)
                        if b == 0:
                            e.wait_ge(s.total, START + 2 * n)
                        e.activation(square[:, HALF * b:HALF * (b + 1), :].rearrange("p h d -> p (h d)"), ps[:, b, :], ACT.Square)\
                            .then_inc(s.square, 1)

                def inverse_norms(l, T, i):
                    n = (l * NT + T) * 2 + i
                    e.wait_ge(s.total, START + 2 * n + 2)
                    e.activation(norm[:, 1, :], norm[:, 0, :], ACT.Ln, bias=const[:, 0:1], scale=LN_RANGE).then_inc(s.root, 1)
                    e.wait_ge(s.root, 2 * n + 1)
                    e.activation(norm[:, 2, :], norm[:, 1, :], ACT.Exp, bias=const[:, 1:2], scale=-0.5).then_inc(s.root, 1)

                def store_values(l, T):
                    e.wait_ge(s.a_ready, START + (l * NT + T) * 6 + 6)
                    e.copy(V[:, T % 3, :, 0:LD], flat2(ps[:, 0:2, :]).rearrange("p (h d) -> p h d", h=LH))\
                        .then_inc(s.v_done, 1)

                def store_qk(l, T, r):
                    n = l * (6 * NT) + turn_index(T, r)
                    e.wait_ge(s.t_ready, n + 1)
                    j0 = 4 * (r % 2)
                    if r < 2:
                        bank = ps[:, 2, :].rearrange("p (j q) -> p j q", j=4)
                        e.copy(qT[0:LD, T % 2, j0:j0 + 4, 0, :], bank[0:LD, :, :])
                        e.copy(qT[LD:P, T % 2, j0:j0 + 4, 1, :], bank[LD:P, :, :]).then_inc(s.t_free, 1)
                    else:
                        e.copy(kT[:, T % 2, j0:j0 + 4, WIN:WIN + P], ps[:, 2, :].rearrange("p (j n) -> p j n", j=4))\
                            .then_inc(s.t_free, 1)
                    if r == 3 and T + 1 < NT:
                        e.wait_ge(s.t_free, START + n + 1)
                        e.activation(kT[:, (T + 1) % 2, :, 0:WIN], kT[:, T % 2, :, P:P + WIN], ACT.Copy,
                                     scale=const[:, 3:4] if (T + 1) % TC == 0 else 1.0)

                def store_o(l, T, r):
                    n = l * (6 * NT) + turn_index(T, r)
                    e.wait_ge(s.t_ready, n + 1)
                    j0 = 4 * (r - 4)
                    e.copy(oT[:, j0:j0 + 4, :].rearrange("p j n -> p (j n)"), ps[:, 2, :]).then_inc(s.t_free, 1)

                def exp(l, T, g):
                    n = (l * NT + T) * LG + g
                    e.wait_ge(s.st_ready, n + 1)
                    e.wait_ge(s.pv_done, START + n)
                    e.activation(weights[:, g % 2, :], ps[:, 5 + g % 2, :], ACT.Exp).then_inc(s.exp_done, 1)

                def square_centred(l, c):
                    cols = slice(c * CH, (c + 1) * CH)
                    e.wait_ge(s.centred, l * NC + c + 1)
                    e.activation(ln_square[:, cols], xn[:, cols], ACT.Square).then_inc(s.ln_sq, 1)

                def inverse_deviation(l, c):
                    cols = slice(c * CH, (c + 1) * CH)
                    e.wait_ge(s.varied, l * NC + c + 1)
                    e.activation(ln_rstd[:, cols], ps[:, VAR_BANK[c], :], ACT.Ln, bias=const[:, 2:3]).then_inc(s.log, 1)
                    e.wait_ge(s.log, l * NC + c + 1)
                    e.activation(ln_rstd[:, cols], ln_rstd[:, cols], ACT.Exp, scale=-0.5).then_inc(s.rstd, 1)

                def attend(l):
                    for T in range(NT):
                        ahead = T + 1 < NT
                        if T:
                            store_o(l, T - 1, 4)
                        if ahead:
                            squares(l, T + 1, 0)
                        if T:
                            store_o(l, T - 1, 5)
                        if ahead:
                            inverse_norms(l, T + 1, 0)
                        if T:
                            e.wait_ge(s.prev_ready, l * (NT - 1) + T)
                            e.wait_ge(s.pv_done, START + (l * NT + T) * LG + 1)
                            e.activation(before[P - WIN:P, :], ps[P - WIN:P, 3, :], ACT.Exp).then_inc(s.prev_done, 1)
                        exp(l, T, 0)
                        if ahead:
                            squares(l, T + 1, 1)
                        exp(l, T, 1)
                        if ahead:
                            inverse_norms(l, T + 1, 1)
                            store_qk(l, T + 1, 0)
                        else:
                            square_centred(l, 0)
                            square_centred(l, 1)
                        exp(l, T, 2)
                        if ahead:
                            store_qk(l, T + 1, 1)
                            store_values(l, T + 1)
                        exp(l, T, 3)
                        if not ahead:
                            square_centred(l, 2)
                        if ahead:
                            store_qk(l, T + 1, 2)
                            store_qk(l, T + 1, 3)
                    store_o(l, NT - 1, 4)
                    store_o(l, NT - 1, 5)

                def gelu_of(l, c, k):
                    n = l * NC + c
                    e.wait_ge(s.gate, n * MT + k + 1)
                    if c:
                        e.wait_ge(s.hidden, (n - 1) * MT + k + 1)
                    e.activation(gelu[0:rows(k), k, :], ps[0:rows(k), 3 + 2 * ((c * MT + k) % 2), :], ACT.Gelu,
                                 bias=b_1[0:rows(k), 1, k:k + 1]).then_inc(s.gelu, 1)

                def forward(l, following):
                    for c in range(NC - 1):
                        inverse_deviation(l, c)
                    square_centred(l, NC - 1)
                    inverse_deviation(l, NC - 1)
                    for c in range(NC):
                        for k in range(MT):
                            gelu_of(l, c, k)
                        if following and c >= NC - 2:
                            e.preload_act_table_set(LN_EXP)
                            squares(l + 1, 0, c - (NC - 2))
                            inverse_norms(l + 1, 0, c - (NC - 2))
                    if following:
                        store_values(l + 1, 0)
                        for r in range(4):
                            store_qk(l + 1, 0, r)

                e.preload_act_table_set(LN_EXP)
                for i in range(2):
                    squares(0, 0, i)
                    inverse_norms(0, 0, i)
                store_values(0, 0)
                for r in range(4):
                    store_qk(0, 0, r)
                with e.Fori(0, DEPTH - 1) as l:
                    e.preload_act_table_set(LN_EXP)
                    attend(l)
                    forward(l, True)
                attend(DEPTH - 1)
                forward(DEPTH - 1, False)

            @block.vector
            def _(e):
                for signal in (s.xs, s.cosine, s.d_free, s.normed, s.total):
                    e.sem_inc(signal, START)

                def sum_squares(l, T, i):
                    n = (l * NT + T) * 2 + i
                    for b in range(2):
                        heads = slice(HALF * b, HALF * (b + 1))
                        e.wait_ge(s.square, 2 * n + b + 1)
                        e.tensor_reduce(norm[:, 0, heads], square[:, heads, :], AX.X, ALU.add).then_inc(s.total, 1)

                def normalise(l, T, i):
                    n = (l * NT + T) * 2 + i
                    e.wait_ge(s.root, 2 * n + 2)
                    e.tensor_scalar(norm[:, 3, :], norm[:, 2, :], 1.0 / NORM_MIN, None, ALU.min).then_inc(s.bound, 1)
                    e.wait_ge(s.bound, n + 1)
                    for b in range(2):
                        heads = slice(HALF * b, HALF * (b + 1))
                        e.tensor_tensor(qn[:, i, heads, :], ps[:, b, :].rearrange("p (h d) -> p h d", h=HALF),
                                        norm[:, 3, heads].unsqueeze(2).to_broadcast([P, HALF, LD]), ALU.mult).then_inc(s.qn, 1)
                    e.wait_ge(s.qn, 2 * n + 2)
                    if T == 0 and i == 0:
                        e.wait_ge(s.tab, START + (l + 1) * 4)
                    e.tensor_tensor(cosine[:, i, :, :], qn[:, i, :, :],
                                    tab[:, 2 * i, T, :].unsqueeze(1).to_broadcast([P, LH, LD]), ALU.mult).then_inc(s.cosine, 1)

                def add_rotated(l, T):
                    n = (l * NT + T) * 2 + 1
                    e.wait_ge(s.rotated, START + n * 3 + 2)
                    e.wait_ge(s.cosine, START + n + 1)
                    e.tensor_tensor(hat[:, 1, :].rearrange("p (h d) -> p h d", h=LH), cosine[:, 1, :, :], sine[:, :, :], ALU.add)\
                        .then_inc(s.rotated, 1)

                def halve(l, T, r):
                    e.wait_ge(s.t_free, START + l * (6 * NT) + turn_index(T, r) + 1)
                    j = slice(4 * (r % 2), 4 * (r % 2) + 4)
                    if r < 2:
                        blocks = qTb[:, T % 2, j, :].rearrange("p j (w two q) -> p j w two q", two=2, q=WIN)
                        for i, half in ((0, slice(0, LD)), (1, slice(LD, P))):
                            ins = e.tensor_copy(blocks[half, :, :, i, :],
                                                qT[half, T % 2, j, i, :].rearrange("p j (w q) -> p j w q", q=WIN))
                    else:
                        ins = e.tensor_copy(kTb[:, T % 2, j, :], kT[:, T % 2, j, :])
                    ins.then_inc(s.half, 1)

                def maxima(l, T, r):
                    n = l * (4 * NT) + d_index(T, r)
                    e.wait_ge(s.d_ready, START + n + 1)
                    e.tensor_reduce(nmax[:, 8 * r:8 * r + 8], ps[:, 3 + r, :].rearrange("p (h k) -> p h k", h=8), AX.X, ALU.max,
                                    negate=True).then_inc(s.d_free, 1)

                def max_rows(l, T):
                    n = l * (4 * NT) + d_index(T, 2)
                    m = l * NT + T
                    e.wait_ge(s.d_ready, START + n + 1)
                    e.wait_ge(mrow_stored[T % 2], START + (l * (NT // 2) + T // 2) * 32)
                    e.tensor_copy(msplit[:, T % 2, 0, :], ps[0:LH, 4, 0:P]).then_inc(s.split, 1)
                    e.wait_ge(s.split, m + 1)
                    e.tensor_tensor(msplit[:, T % 2, 1, :], ps[0:LH, 4, 0:P], msplit[:, T % 2, 0, :], ALU.subtract)\
                        .then_inc(s.d_free, 1)

                def residual(l, T):
                    n = l * (4 * NT) + d_index(T, 3)
                    e.wait_ge(s.d_ready, START + n + 1)
                    e.tensor_tensor(X[:, T * P:(T + 1) * P], X[:, T * P:(T + 1) * P], ps[:, 4, 0:P], ALU.add)\
                        .then_inc(s.d_free, 1)

                def outputs(l, T, g):
                    n = (l * NT + T) * LG + g
                    e.wait_ge(s.pv_done, START + n + 2)
                    m = ps[:, VALUE_BANK[g], 0:QG * VL].rearrange("p (h w) -> p h w", h=QG)
                    e.reciprocal(rcp[:, :], m[:, :, LD]).then_inc(s.rcp, 1)
                    e.wait_ge(s.rcp, n + 1)
                    e.tensor_tensor(o_tok[:, T % 2, QG * g:QG * (g + 1), :], m[:, :, 0:LD],
                                    rcp[:, :].unsqueeze(2).to_broadcast([P, QG, LD]), ALU.mult).then_inc(s.normed, 1)
                    e.wait_ge(s.normed, START + n + 1)

                def shift(c, signal):
                    lo, hi = c * CH, (c + 1) * CH
                    e.tensor_copy(XS[0:P // 2, lo:hi], X[0:P // 2, lo:hi]).then_inc(signal, 1)
                    lo = max(lo, 1)
                    e.tensor_copy(XS[P // 2:P, lo:hi], X[P // 2:P, lo - 1:hi - 1]).then_inc(signal, 1)

                def centre(l, c):
                    cols = slice(c * CH, (c + 1) * CH)
                    e.wait_ge(s.xs, START + l * SHIFTS + 2 * c + 2)
                    e.wait_ge(s.mean, l * NC + c + 1)
                    e.tensor_tensor(xn[:, cols], XS[:, cols], ps[:, MEAN_BANK[c], :], ALU.subtract).then_inc(s.centred, 1)

                def attend(l):
                    for T in range(NT):
                        ahead = T + 1 < NT
                        maxima(l, T, 0)
                        maxima(l, T, 1)
                        max_rows(l, T)
                        if ahead:
                            sum_squares(l, T + 1, 0)
                            normalise(l, T + 1, 0)
                        if T:
                            residual(l, T - 1)
                        if ahead:
                            sum_squares(l, T + 1, 1)
                        else:
                            e.wait_ge(s.d_free, START + l * (4 * NT) + d_index(NT - 2, 3) + 1)
                            for c in range(NC - 1):
                                shift(c, s.xs)
                            centre(l, 0)
                            centre(l, 1)
                        outputs(l, T, 0)
                        if ahead:
                            normalise(l, T + 1, 1)
                            halve(l, T + 1, 0)
                        outputs(l, T, 1)
                        if ahead:
                            add_rotated(l, T + 1)
                            halve(l, T + 1, 1)
                        else:
                            centre(l, 2)
                        outputs(l, T, 2)
                        if ahead:
                            halve(l, T + 1, 2)
                            halve(l, T + 1, 3)
                        outputs(l, T, 3)
                    residual(l, NT - 1)
                    e.wait_ge(s.d_free, START + (l + 1) * (4 * NT))

                def hide(l, c, k):
                    n = l * NC + c
                    e.wait_ge(s.gelu, n * MT + k + 1)
                    e.wait_ge(s.up, n * MT + k + 1)
                    e.scalar_tensor_tensor(out=hidden[0:rows(k), k, :], in0=ps[0:rows(k), 4 + 2 * ((c * MT + k) % 2), :],
                                           scalar=b_1[0:rows(k), 0, k:k + 1], in1=gelu[0:rows(k), k, :],
                                           op0=ALU.add, op1=ALU.mult).then_inc(s.hidden, 1)

                def add_output(l, c):
                    n = l * NC + c
                    lo, hi = c * CH, (c + 1) * CH
                    e.wait_ge(s.y, n + 1)
                    e.scalar_tensor_tensor(out=X[:, lo:hi], in0=ps[:, 7, :], scalar=vec[:, 2:3], in1=X[:, lo:hi],
                                           op0=ALU.add, op1=ALU.add).then_inc(s.summed, 1)
                    e.wait_ge(s.summed, n + 1)
                    shift(c, s.xs)

                def forward(l, following):
                    shift(NC - 1, s.xs)
                    e.wait_ge(s.w_mlp, (l + 1) * 192)
                    for c in range(NC):
                        n = l * NC + c
                        cols = slice(c * CH, (c + 1) * CH)
                        if c == 1:
                            centre(l, NC - 1)
                        e.wait_ge(s.rstd, n + 1)
                        e.scalar_tensor_tensor(out=xn[:, cols], in0=xn[:, cols], scalar=vec[:, 0:1], in1=ln_rstd[:, cols],
                                               op0=ALU.mult, op1=ALU.mult).then_inc(s.xn, 1)
                        e.wait_ge(s.xn, 2 * n + 1)
                        e.tensor_scalar(xn[:, cols], xn[:, cols], vec[:, 1:2], None, ALU.add).then_inc(s.xn, 1)
                    for c in range(NC):
                        if c:
                            add_output(l, c - 1)
                        for k in range(MT):
                            hide(l, c, k)
                        if following and c >= NC - 2:
                            sum_squares(l + 1, 0, c - (NC - 2))
                            normalise(l + 1, 0, c - (NC - 2))
                    add_output(l, NC - 1)
                    e.wait_ge(s.xs, START + (l + 1) * SHIFTS)
                    if following:
                        add_rotated(l + 1, 0)
                        for r in range(4):
                            halve(l + 1, 0, r)

                for i in range(2):
                    sum_squares(0, 0, i)
                    normalise(0, 0, i)
                add_rotated(0, 0)
                for r in range(4):
                    halve(0, 0, r)
                with e.Fori(0, DEPTH - 1) as l:
                    attend(l)
                    forward(l, True)
                attend(DEPTH - 1)
                forward(DEPTH - 1, False)


def tables():
    import numpy as np
    bf16 = mybir.dt.np(mybir.dt.bfloat16)
    ident = np.eye(P, dtype=np.float32)
    i = np.arange(P)
    inv = (1.0 / 10000.0 ** (np.arange(0, HD, 2, dtype=np.float32) / np.float32(HD))).astype(np.float32)
    freq = (np.arange(N, dtype=np.float32)[:, None] * inv[None, :]).astype(np.float32)
    rope = lambda f: np.ascontiguousarray(np.tile(np.repeat(f(freq), 2, axis=1), (1, H)).T.astype(np.float32))
    mask = np.where(i[None, :] > i[:, None], -1e30, 0.0)
    half = np.arange(0, LD, 2, dtype=np.float32)
    token = np.arange(N, dtype=np.float32)
    lfreq = token[:, None] * (1.0 / 10000.0 ** (half / np.float32(LD))).astype(np.float32)[None, :]
    lfreq = np.concatenate([lfreq, lfreq], -1).astype(np.float32)
    growth = ((half + 0.4 * LD) / (1.4 * LD)).astype(np.float64)
    growth = np.concatenate([growth, growth])
    power = (token % CH - CH // 2).astype(np.float64) / (WIN // 2)
    scale = growth[None, :] ** power[:, None]
    sign = np.where(np.arange(LD) < ROT, -1.0, 1.0)
    cos, sin = np.cos(lfreq), np.sin(lfreq) * sign
    base = np.stack([cos * scale * QK_SCALE, sin * scale * QK_SCALE, cos / scale, sin / scale]).astype(np.float32)
    base = np.ascontiguousarray(base.reshape(4, NT, P, LD).transpose(2, 0, 1, 3))
    key = np.arange(2 * WIN)[None, :]
    query = (i % WIN)[:, None]
    seen = (query <= key) & (key <= query + WIN)
    seen0 = seen & ((i[:, None] >= 2 * WIN) | (key >= WIN))
    low = lambda m: np.where(m, 0.0, -1e30)
    mask_c = np.stack([np.tile(low(seen), (1, 8)), np.tile(np.concatenate([low(seen0), low(seen)], 1), (1, 4))], 1)
    ahead = i[None, :] - i[:, None]
    mask_d = np.tile(low((ahead >= 0) & (ahead <= WIN)), (1, QG))
    mask_p = np.zeros((P, LH * WIN))
    mask_p[P - WIN:] = np.tile(low(np.arange(WIN)[None, :] <= np.arange(WIN)[:, None]), (1, LH))
    const = np.zeros((P, 4), np.float32)
    const[:, 0], const[:, 1], const[:, 2] = LN_TINY, 0.5 * np.log(LN_RANGE), EPS
    const[:, 3] = growth[i % LD] ** (CH // (WIN // 2))
    return {
        "c_base": base, "c_mask_c": mask_c.astype(bf16), "c_mask_d": mask_d.astype(bf16),
        "c_mask_p": mask_p.astype(bf16), "c_const": const,
        "c_ident": ident, "c_identb": ident.astype(bf16),
        "c_mask_qk": mask.astype(bf16), "c_mask_kq": np.ascontiguousarray(mask.T).astype(bf16),
        "c_cos": rope(np.cos), "c_sin": rope(np.sin),
    }


def program(nc, a, out):
    with ExitStack() as outer:
        t, d = Names(), Names()
        sbo = lambda name, shape, dt=F32: outer.enter_context(nc.sbuf_tensor(name, shape, dt))
        t.x = sbo("x", [P, NT, P])
        t.X = sbo("X", [P, N])
        t.ident = sbo("ident", [P, P])
        t.stat = sbo("stat", [P, 48])
        t.identb = sbo("identb", [P, P], BF16)
        t.ps = outer.enter_context(nc.psum_tensor("ps", [P, 8, CH], F32))
        d.rope_cos, d.rope_sin = a["c_cos"], a["c_sin"]
        d.pieces = nc.dram_tensor("pieces", [2, 3, P, N], BF16).ap()
        rows = lambda x: x.rearrange("a (t p) n -> (a p) t n", p=P)
        with ExitStack() as ctx:
            sb = lambda name, shape, dt=F32: ctx.enter_context(nc.sbuf_tensor(name, shape, dt))
            t.V = sb("V", [P, NT, H * VW + 32 - VW])
            t.mask_qk = sb("mask_qk", [P, P], BF16)
            t.mask_kq = sb("mask_kq", [P, P], BF16)
            t.wo = sb("wo", [P, P])
            loaded = ctx.enter_context(nc.semaphore("loaded"))
            with nc.Block() as block:
                @block.sync
                def _(e):
                    e.dma_start(t.x[:, :, :], rows(a["L0_attn_x"])).then_inc(loaded, 16)
                    e.dma_start(t.ident[:, :], a["c_ident"]).then_inc(loaded, 16)
                    e.dma_start(t.identb[:, :], a["c_identb"]).then_inc(loaded, 16)
                    e.dma_start(t.mask_qk[:, :], a["c_mask_qk"]).then_inc(loaded, 16)
                    e.dma_start(t.mask_kq[:, :], a["c_mask_kq"]).then_inc(loaded, 16)
                    e.wait_ge(loaded, 80)
            w = a["L0_attn_w_qkv"]
            attention_inputs(nc, t, "a0_", d, [w[:, i * P:(i + 1) * P] for i in range(3)], a["L0_attn_w_proj"], False)
            attention(nc, t, "a0_", d, False)
            fp4_feed_forward(nc, t, a)
            attention_inputs(nc, t, "a1_", d, [a["L1_attn_Wq"], a["L1_attn_Wk"], a["L1_attn_Wv"]], a["L1_attn_Wo"], True)
            attention(nc, t, "a1_", d, True)
        layers(nc, t, a)
        with ExitStack() as ctx:
            s = semaphores(ctx, nc, "end_", "transposed copied stored")
            with nc.Block() as block:
                @block.tensor
                def _(e):
                    for i in range(NT):
                        e.transpose(t.ps[:, i // TC, (i % TC) * P:(i % TC + 1) * P], t.X[:, i * P:(i + 1) * P],
                                    t.ident[:, :]).then_inc(s.transposed, 1)

                @block.vector
                def _(e):
                    for c in range(NC):
                        e.wait_ge(s.transposed, TC * (c + 1))
                        e.tensor_tensor(t.x[:, TC * c:TC * (c + 1), :], t.x[:, TC * c:TC * (c + 1), :],
                                        t.ps[:, c, :].rearrange("p (q n) -> p q n", q=TC), ALU.add)\
                            .then_inc(s.copied, 1)

                @block.sync
                def _(e):
                    for c in range(NC):
                        e.wait_ge(s.copied, c + 1)
                        e.dma_start(rows(out)[:, TC * c:TC * (c + 1), :], t.x[:, TC * c:TC * (c + 1), :]).then_inc(s.stored, 16)
                    e.wait_ge(s.stored, 16 * NC)


_INS = ["L0_attn_x", "L0_attn_w_qkv", "L0_attn_w_proj", "L0_ffn_w_gate", "L0_ffn_w_up", "L0_ffn_w_down", "L1_attn_Wq",
        "L1_attn_Wk", "L1_attn_Wv", "L1_attn_Wo", "L1_ffn_Wqkv", "L1_ffn_q_scale", "L1_ffn_k_scale", "L1_ffn_Wo",
        "L1_ffn_ln_g", "L1_ffn_ln_b", "L1_ffn_W1", "L1_ffn_b1", "L1_ffn_W2", "L1_ffn_b2"]


def kernel(**inputs):
    import numpy as np
    import concourse.bacc as bacc
    from concourse.bass_utils import run_bass_kernel_spmd

    nc = bacc.Bacc("TRN2", target_bir_lowering=False, num_devices=1)
    arrays = {name: np.ascontiguousarray(inputs[name]) for name in _INS}
    arrays.update(tables())
    named = {f"in_{name}_dram": value for name, value in arrays.items()}
    a = {name: nc.dram_tensor(f"in_{name}_dram", value.shape, mybir.dt.from_np(value.dtype), kind="ExternalInput").ap()
         for name, value in arrays.items()}
    out = nc.dram_tensor("out_0_dram", (1, N, P), F32, kind="ExternalOutput").ap()
    program(nc, a, out)
    r = run_bass_kernel_spmd(nc, [named], core_ids=[0])
    return r.results[0]["out_0_dram"]
```
